# Optimizing a Trainium2 kernel written in Bass

```python
import numpy as np
import jax
import jax.numpy as jnp

def _softmax(x, axis=-1):
    return jax.nn.softmax(x, axis=axis)

def _gelu(x):
    return jax.nn.gelu(x, approximate=True)

def _silu(x):
    return jax.nn.silu(x)

def _sigmoid(x):
    return jax.nn.sigmoid(x)

def _layernorm(x, axis=-1, eps=1e-05):
    m = jnp.mean(x, axis=axis, keepdims=True)
    v = jnp.var(x, axis=axis, keepdims=True)
    return (x - m) / jnp.sqrt(v + eps)

def _scatter_add(tgt, idx, src, axis=0):
    return tgt.at[idx].add(src)

def _segment_sum(src, seg, n):
    return jax.ops.segment_sum(src, seg, n)
kernel_name = 'mk_hybrid_d1_jaxref_r8_bfa141'

def setup_inputs(seed: int=0):
    np.random.seed(seed)
    _w = jnp.asarray

    def _L0_attn_a_setup():
        import jax, jax.numpy as jnp
        import numpy as np
        B, T, K, H = (2, 256, 128, 16)
        key = jax.random.key(seed)
        ks = jax.random.split(key, 9)
        sc = 0.02
        return {'x': jax.random.normal(ks[0], (B, T, K), dtype=jnp.float32), 'Wq_w': jax.random.normal(ks[1], (K, K), dtype=jnp.float32) * sc, 'Wq_b': jax.random.normal(ks[2], (K,), dtype=jnp.float32) * sc, 'Wk_w': jax.random.normal(ks[3], (K, K), dtype=jnp.float32) * sc, 'Wk_b': jax.random.normal(ks[4], (K,), dtype=jnp.float32) * sc, 'Wv_w': jax.random.normal(ks[5], (K, K), dtype=jnp.float32) * sc, 'Wv_b': jax.random.normal(ks[6], (K,), dtype=jnp.float32) * sc, 'Wo_w': jax.random.normal(ks[7], (K, K), dtype=jnp.float32) * sc, 'Wo_b': jax.random.normal(ks[8], (K,), dtype=jnp.float32) * sc}
    _L0_attn_a_in = _L0_attn_a_setup()

    def _L0_attn_b_setup():
        import jax, jax.numpy as jnp
        import numpy as np
        H = 4
        DK = 32
        DV = 32
        M = 32
        GATE_NORM = 16.0
        EPS = 1e-05

        def _rmsnorm(x, w):
            var = jnp.mean(jnp.square(x), axis=-1, keepdims=True)
            return x * jax.lax.rsqrt(var + EPS) * w

        def _swish(x):
            return x * jax.nn.sigmoid(x)

        def _gsa_scan(q, k, v, s, g):
            B, Hh = (q.shape[1], q.shape[2])
            Hk0 = jnp.zeros((B, Hh, DK, M), q.dtype)
            Hv0 = jnp.zeros((B, Hh, M, DV), q.dtype)

            def step(carry, xs):
                Hk, Hv = carry
                qt, kt, vt, st, gt = xs
                lam = jnp.exp(gt)
                Hk = Hk * lam[:, :, None, :] + kt[..., :, None] * st[..., None, :]
                z = jnp.einsum('bhk,bhkm->bhm', qt, Hk)
                p = jax.nn.softmax(z, axis=-1)
                Hv = Hv * lam[..., :, None] + st[..., :, None] * vt[..., None, :]
                ot = jnp.einsum('bhm,bhmv->bhv', p, Hv)
                return ((Hk, Hv), ot)
            _, o = jax.lax.scan(step, (Hk0, Hv0), (q, k, v, s, g))
            return o
        key = jax.random.key(seed)
        ks = jax.random.split(key, 8)
        B, T, D = (4, 256, 128)
        scale = 2 ** (-2.5) * (2.0 / (D + D)) ** 0.5 * 3.0 ** 0.5 * 2
        return {'hidden_states': jax.random.normal(ks[0], (B, T, D), jnp.float32), 'norm_weight': jnp.ones((D,), jnp.float32), 'w_q': jax.random.normal(ks[1], (D, D), jnp.float32) * scale, 'w_k': jax.random.normal(ks[2], (D, D), jnp.float32) * scale, 'w_v': jax.random.normal(ks[3], (D, D), jnp.float32) * scale, 'w_f': jax.random.normal(ks[4], (H * M, D), jnp.float32) * scale, 'gnorm_weight': jnp.ones((D,), jnp.float32), 'w_o': jax.random.normal(ks[5], (D, D), jnp.float32) * scale}
    _L0_attn_b_in = _L0_attn_b_setup()

    def _L0_ffn_setup():
        import jax, jax.numpy as jnp
        import numpy as np
        DIM = 128
        DEPTH = 6
        HEADS = 16
        DIM_HEAD = 64
        WINDOW = 32
        INNER = HEADS * DIM_HEAD
        DIM_INNER = int(DIM * 4 * 2 / 3)
        QK_SCALE = 8.0

        def shift_tokens(t):
            a, s = jnp.split(t, 2, -1)
            s = jnp.pad(s, ((0, 0), (1, 0), (0, 0)))[:, :-1]
            return jnp.concatenate([a, s], -1)

        def l2norm(t):
            return t / jnp.maximum(jnp.linalg.norm(t, axis=-1, keepdims=True), 1e-12)

        def rotate_half(x):
            x1, x2 = jnp.split(x, 2, -1)
            return jnp.concatenate([-x2, x1], -1)

        def rotary_tables(n):
            half = jnp.arange(0, DIM_HEAD, 2, dtype=jnp.float32)
            inv_freq = 1.0 / 10000.0 ** (half / DIM_HEAD)
            t = jnp.arange(n, dtype=jnp.float32)
            freqs = t[:, None] * inv_freq[None, :]
            freqs = jnp.concatenate([freqs, freqs], -1)
            base_scale = (half + 0.4 * DIM_HEAD) / (1.4 * DIM_HEAD)
            power = (t - n // 2) / (WINDOW // 2)
            scale = base_scale[None, :] ** power[:, None]
            scale = jnp.concatenate([scale, scale], -1)
            return (freqs, scale)

        def local_attention(q, k, v):
            b, h, n, d = q.shape
            w = WINDOW
            nw = n // w
            bq = q.reshape(b, h, nw, w, d)
            bk = k.reshape(b, h, nw, w, d)
            bv = v.reshape(b, h, nw, w, d)

            def look(t):
                p = jnp.pad(t, ((0, 0), (0, 0), (1, 0), (0, 0), (0, 0)))
                return jnp.concatenate([p[:, :, :nw], p[:, :, 1:]], axis=3)
            bk2, bv2 = (look(bk), look(bv))
            seq = jnp.arange(n).reshape(nw, w)
            seq_p = jnp.pad(seq, ((1, 0), (0, 0)), constant_values=-1)
            jt = jnp.concatenate([seq_p[:nw], seq_p[1:]], axis=1)
            it = seq[:, :, None]
            jb = jt[:, None, :]
            mask = (it < jb) | (it > jb + w) | (jb == -1)
            sim = jnp.einsum('bhwie,bhwje->bhwij', bq, bk2) * QK_SCALE
            sim = jnp.where(mask, -jnp.finfo(sim.dtype).max, sim)
            attn = jax.nn.softmax(sim, -1)
            out = jnp.einsum('bhwij,bhwje->bhwie', attn, bv2)
            return out.reshape(b, h, n, d)

        def attn_layer(x, Wqkv, qs, ksc, Wo):
            b, n, _ = x.shape
            qkv = x @ Wqkv
            q, k, v = jnp.split(qkv, 3, -1)
            sh = lambda t: t.reshape(b, n, HEADS, DIM_HEAD).transpose(0, 2, 1, 3)
            q, k, v = (sh(q), sh(k), sh(v))
            q = l2norm(q) * qs
            k = l2norm(k) * ksc
            freqs, scale = rotary_tables(n)
            cos, sin = (jnp.cos(freqs), jnp.sin(freqs))
            q = q * cos * scale + rotate_half(q) * sin * scale
            inv = 1.0 / scale
            k = k * cos * inv + rotate_half(k) * sin * inv
            out = local_attention(q, k, v)
            out = out.transpose(0, 2, 1, 3).reshape(b, n, INNER)
            return out @ Wo

        def ffn_layer(x, g, bln, W1, b1, W2, b2):
            mu = x.mean(-1, keepdims=True)
            var = ((x - mu) ** 2).mean(-1, keepdims=True)
            xn = (x - mu) / jnp.sqrt(var + 1e-05) * g + bln
            hg = xn @ W1 + b1
            a, gate = jnp.split(hg, 2, -1)
            return a * jax.nn.gelu(gate, approximate=False) @ W2 + b2
        key = jax.random.key(seed)
        ks = jax.random.split(key, 8)
        B, N = (2, 256)
        init = lambda k, shape: jax.random.normal(k, shape, jnp.float32) * 0.02
        return {'x': jax.random.normal(ks[0], (B, N, DIM), jnp.float32), 'Wqkv': init(ks[1], (DEPTH, DIM, 3 * INNER)), 'q_scale': jnp.ones((DEPTH, DIM_HEAD), jnp.float32), 'k_scale': jnp.ones((DEPTH, DIM_HEAD), jnp.float32), 'Wo': init(ks[2], (DEPTH, INNER, DIM)), 'ln_g': jnp.ones((DEPTH, DIM), jnp.float32), 'ln_b': jnp.zeros((DEPTH, DIM), jnp.float32), 'W1': init(ks[3], (DEPTH, DIM, 2 * DIM_INNER)), 'b1': jnp.zeros((DEPTH, 2 * DIM_INNER), jnp.float32), 'W2': init(ks[4], (DEPTH, DIM_INNER, DIM)), 'b2': jnp.zeros((DEPTH, DIM), jnp.float32)}
    _L0_ffn_in = _L0_ffn_setup()
    _d = {'L0_attn_a_x': _L0_attn_a_in['x'], 'L0_attn_a_Wq_w': _L0_attn_a_in['Wq_w'], 'L0_attn_a_Wq_b': _L0_attn_a_in['Wq_b'], 'L0_attn_a_Wk_w': _L0_attn_a_in['Wk_w'], 'L0_attn_a_Wk_b': _L0_attn_a_in['Wk_b'], 'L0_attn_a_Wv_w': _L0_attn_a_in['Wv_w'], 'L0_attn_a_Wv_b': _L0_attn_a_in['Wv_b'], 'L0_attn_a_Wo_w': _L0_attn_a_in['Wo_w'], 'L0_attn_a_Wo_b': _L0_attn_a_in['Wo_b'], 'L0_attn_b_norm_weight': _L0_attn_b_in['norm_weight'], 'L0_attn_b_w_q': _L0_attn_b_in['w_q'], 'L0_attn_b_w_k': _L0_attn_b_in['w_k'], 'L0_attn_b_w_v': _L0_attn_b_in['w_v'], 'L0_attn_b_w_f': _L0_attn_b_in['w_f'], 'L0_attn_b_gnorm_weight': _L0_attn_b_in['gnorm_weight'], 'L0_attn_b_w_o': _L0_attn_b_in['w_o'], 'L0_ffn_Wqkv': _L0_ffn_in['Wqkv'], 'L0_ffn_q_scale': _L0_ffn_in['q_scale'], 'L0_ffn_k_scale': _L0_ffn_in['k_scale'], 'L0_ffn_Wo': _L0_ffn_in['Wo'], 'L0_ffn_ln_g': _L0_ffn_in['ln_g'], 'L0_ffn_ln_b': _L0_ffn_in['ln_b'], 'L0_ffn_W1': _L0_ffn_in['W1'], 'L0_ffn_b1': _L0_ffn_in['b1'], 'L0_ffn_W2': _L0_ffn_in['W2'], 'L0_ffn_b2': _L0_ffn_in['b2']}
    _x0 = _d['L0_attn_a_x']
    _d['L0_attn_a_x'] = jax.random.normal(jax.random.fold_in(jax.random.key(seed), 1), (2, 1024, 128), dtype=_x0.dtype)
    del _x0
    return _d

def reference(L0_attn_a_x, L0_attn_a_Wq_w, L0_attn_a_Wq_b, L0_attn_a_Wk_w, L0_attn_a_Wk_b, L0_attn_a_Wv_w, L0_attn_a_Wv_b, L0_attn_a_Wo_w, L0_attn_a_Wo_b, L0_attn_b_norm_weight, L0_attn_b_w_q, L0_attn_b_w_k, L0_attn_b_w_v, L0_attn_b_w_f, L0_attn_b_gnorm_weight, L0_attn_b_w_o, L0_ffn_Wqkv, L0_ffn_q_scale, L0_ffn_k_scale, L0_ffn_Wo, L0_ffn_ln_g, L0_ffn_ln_b, L0_ffn_W1, L0_ffn_b1, L0_ffn_W2, L0_ffn_b2):

    def _L0_attn_a_ref(x, Wq_w, Wq_b, Wk_w, Wk_b, Wv_w, Wv_b, Wo_w, Wo_b):
        import jax, jax.numpy as jnp
        import numpy as np
        B, T, K, H = (2, 256, 128, 16)
        b, t, k = x.shape
        h = H
        s = k // h
        q = x @ Wq_w.T + Wq_b
        kk = x @ Wk_w.T + Wk_b
        v = x @ Wv_w.T + Wv_b
        q = q.reshape(b, t, h, s).transpose(0, 2, 1, 3)
        kk = kk.reshape(b, t, h, s).transpose(0, 2, 1, 3)
        v = v.reshape(b, t, h, s).transpose(0, 2, 1, 3)
        dot = jnp.einsum('bhqd,bhkd->bhqk', q, kk)
        causal = jnp.tril(jnp.ones((t, t), dtype=bool))
        dot = jnp.where(causal, dot, -jnp.inf)
        dot = dot / jnp.sqrt(jnp.asarray(k, dot.dtype))
        attn = jax.nn.softmax(dot, axis=-1)
        out = jnp.einsum('bhqk,bhkd->bhqd', attn, v)
        out = out.transpose(0, 2, 1, 3).reshape(b, t, k)
        return out @ Wo_w.T + Wo_b

    def _L0_attn_b_ref(hidden_states, norm_weight, w_q, w_k, w_v, w_f, gnorm_weight, w_o):
        import jax, jax.numpy as jnp
        import numpy as np
        H = 4
        DK = 32
        DV = 32
        M = 32
        GATE_NORM = 16.0
        EPS = 1e-05

        def _rmsnorm(x, w):
            var = jnp.mean(jnp.square(x), axis=-1, keepdims=True)
            return x * jax.lax.rsqrt(var + EPS) * w

        def _swish(x):
            return x * jax.nn.sigmoid(x)

        def _gsa_scan(q, k, v, s, g):
            B, Hh = (q.shape[1], q.shape[2])
            Hk0 = jnp.zeros((B, Hh, DK, M), q.dtype)
            Hv0 = jnp.zeros((B, Hh, M, DV), q.dtype)

            def step(carry, xs):
                Hk, Hv = carry
                qt, kt, vt, st, gt = xs
                lam = jnp.exp(gt)
                Hk = Hk * lam[:, :, None, :] + kt[..., :, None] * st[..., None, :]
                z = jnp.einsum('bhk,bhkm->bhm', qt, Hk)
                p = jax.nn.softmax(z, axis=-1)
                Hv = Hv * lam[..., :, None] + st[..., :, None] * vt[..., None, :]
                ot = jnp.einsum('bhm,bhmv->bhv', p, Hv)
                return ((Hk, Hv), ot)
            _, o = jax.lax.scan(step, (Hk0, Hv0), (q, k, v, s, g))
            return o
        B, T, D = hidden_states.shape
        h = _rmsnorm(hidden_states, norm_weight)
        q = _swish(h @ w_q.T).reshape(B, T, H, DK)
        k = _swish(h @ w_k.T).reshape(B, T, H, DK)
        v = _swish(h @ w_v.T).reshape(B, T, H, DV)
        f = jax.nn.log_sigmoid(h @ w_f.T).reshape(B, T, H, M) / GATE_NORM
        s = 1.0 - jnp.exp(f)
        tm = lambda x: jnp.transpose(x, (1, 0, 2, 3))
        o = _gsa_scan(tm(q), tm(k), tm(v), tm(s), tm(f))
        o = jnp.transpose(o, (1, 0, 2, 3)).reshape(B, T, H * DV)
        o = _swish(o)
        o = _rmsnorm(o, gnorm_weight)
        return o @ w_o.T

    def _L0_ffn_ref(x, Wqkv, q_scale, k_scale, Wo, ln_g, ln_b, W1, b1, W2, b2):
        import jax, jax.numpy as jnp
        import numpy as np
        DIM = 128
        DEPTH = 6
        HEADS = 16
        DIM_HEAD = 64
        WINDOW = 32
        INNER = HEADS * DIM_HEAD
        DIM_INNER = int(DIM * 4 * 2 / 3)
        QK_SCALE = 8.0

        def shift_tokens(t):
            a, s = jnp.split(t, 2, -1)
            s = jnp.pad(s, ((0, 0), (1, 0), (0, 0)))[:, :-1]
            return jnp.concatenate([a, s], -1)

        def l2norm(t):
            return t / jnp.maximum(jnp.linalg.norm(t, axis=-1, keepdims=True), 1e-12)

        def rotate_half(x):
            x1, x2 = jnp.split(x, 2, -1)
            return jnp.concatenate([-x2, x1], -1)

        def rotary_tables(n):
            half = jnp.arange(0, DIM_HEAD, 2, dtype=jnp.float32)
            inv_freq = 1.0 / 10000.0 ** (half / DIM_HEAD)
            t = jnp.arange(n, dtype=jnp.float32)
            freqs = t[:, None] * inv_freq[None, :]
            freqs = jnp.concatenate([freqs, freqs], -1)
            base_scale = (half + 0.4 * DIM_HEAD) / (1.4 * DIM_HEAD)
            power = (t - n // 2) / (WINDOW // 2)
            scale = base_scale[None, :] ** power[:, None]
            scale = jnp.concatenate([scale, scale], -1)
            return (freqs, scale)

        def local_attention(q, k, v):
            b, h, n, d = q.shape
            w = WINDOW
            nw = n // w
            bq = q.reshape(b, h, nw, w, d)
            bk = k.reshape(b, h, nw, w, d)
            bv = v.reshape(b, h, nw, w, d)

            def look(t):
                p = jnp.pad(t, ((0, 0), (0, 0), (1, 0), (0, 0), (0, 0)))
                return jnp.concatenate([p[:, :, :nw], p[:, :, 1:]], axis=3)
            bk2, bv2 = (look(bk), look(bv))
            seq = jnp.arange(n).reshape(nw, w)
            seq_p = jnp.pad(seq, ((1, 0), (0, 0)), constant_values=-1)
            jt = jnp.concatenate([seq_p[:nw], seq_p[1:]], axis=1)
            it = seq[:, :, None]
            jb = jt[:, None, :]
            mask = (it < jb) | (it > jb + w) | (jb == -1)
            sim = jnp.einsum('bhwie,bhwje->bhwij', bq, bk2) * QK_SCALE
            sim = jnp.where(mask, -jnp.finfo(sim.dtype).max, sim)
            attn = jax.nn.softmax(sim, -1)
            out = jnp.einsum('bhwij,bhwje->bhwie', attn, bv2)
            return out.reshape(b, h, n, d)

        def attn_layer(x, Wqkv, qs, ksc, Wo):
            b, n, _ = x.shape
            qkv = x @ Wqkv
            q, k, v = jnp.split(qkv, 3, -1)
            sh = lambda t: t.reshape(b, n, HEADS, DIM_HEAD).transpose(0, 2, 1, 3)
            q, k, v = (sh(q), sh(k), sh(v))
            q = l2norm(q) * qs
            k = l2norm(k) * ksc
            freqs, scale = rotary_tables(n)
            cos, sin = (jnp.cos(freqs), jnp.sin(freqs))
            q = q * cos * scale + rotate_half(q) * sin * scale
            inv = 1.0 / scale
            k = k * cos * inv + rotate_half(k) * sin * inv
            out = local_attention(q, k, v)
            out = out.transpose(0, 2, 1, 3).reshape(b, n, INNER)
            return out @ Wo

        def ffn_layer(x, g, bln, W1, b1, W2, b2):
            mu = x.mean(-1, keepdims=True)
            var = ((x - mu) ** 2).mean(-1, keepdims=True)
            xn = (x - mu) / jnp.sqrt(var + 1e-05) * g + bln
            hg = xn @ W1 + b1
            a, gate = jnp.split(hg, 2, -1)
            return a * jax.nn.gelu(gate, approximate=False) @ W2 + b2
        for i in range(DEPTH):
            x = attn_layer(shift_tokens(x), Wqkv[i], q_scale[i], k_scale[i], Wo[i]) + x
            x = ffn_layer(shift_tokens(x), ln_g[i], ln_b[i], W1[i], b1[i], W2[i], b2[i]) + x
        return x
    x = L0_attn_a_x
    x = x + _L0_attn_a_ref(_layernorm(x, axis=-1), L0_attn_a_Wq_w, L0_attn_a_Wq_b, L0_attn_a_Wk_w, L0_attn_a_Wk_b, L0_attn_a_Wv_w, L0_attn_a_Wv_b, L0_attn_a_Wo_w, L0_attn_a_Wo_b)
    x = x + _L0_ffn_ref(_layernorm(x, axis=-1), L0_ffn_Wqkv, L0_ffn_q_scale, L0_ffn_k_scale, L0_ffn_Wo, L0_ffn_ln_g, L0_ffn_ln_b, L0_ffn_W1, L0_ffn_b1, L0_ffn_W2, L0_ffn_b2)
    x = x + _L0_attn_b_ref(_layernorm(x, axis=-1), L0_attn_b_norm_weight, L0_attn_b_w_q, L0_attn_b_w_k, L0_attn_b_w_v, L0_attn_b_w_f, L0_attn_b_gnorm_weight, L0_attn_b_w_o)
    x = x + _L0_ffn_ref(_layernorm(x, axis=-1), L0_ffn_Wqkv, L0_ffn_q_scale, L0_ffn_k_scale, L0_ffn_Wo, L0_ffn_ln_g, L0_ffn_ln_b, L0_ffn_W1, L0_ffn_b1, L0_ffn_W2, L0_ffn_b2)
    return x

_drawn_inputs = setup_inputs


def setup_inputs(seed=0):
    import zlib

    import numpy as np

    out = dict(_drawn_inputs(seed))
    spreads = {'L0_attn_b_norm_weight': (1.0, 0.2),
     'L0_attn_b_gnorm_weight': (1.0, 0.2),
     'L0_ffn_q_scale': (1.0, 0.6),
     'L0_ffn_k_scale': (1.0, 0.6),
     'L0_ffn_ln_g': (1.0, 0.6),
     'L0_ffn_ln_b': (0.0, 0.8),
     'L0_ffn_b1': (0.0, 0.585),
     'L0_ffn_b2': (0.0, 0.1)}
    factors = {'L0_attn_a_Wq_w': 8.0,
     'L0_attn_a_Wq_b': 8.0,
     'L0_attn_a_Wk_w': 8.0,
     'L0_attn_a_Wk_b': 8.0,
     'L0_attn_a_Wv_w': 8.0,
     'L0_attn_a_Wv_b': 8.0,
     'L0_attn_a_Wo_w': 6.645,
     'L0_attn_b_w_q': 8.0,
     'L0_attn_b_w_k': 8.0,
     'L0_attn_b_w_f': 4.135}
    for name, (base, spread) in spreads.items():
        noise = np.random.default_rng([zlib.crc32(name.encode()), seed]).standard_normal(out[name].shape)
        drawn = base * np.exp(spread * noise) if base else spread * noise
        out[name] = jnp.asarray(drawn.astype(out[name].dtype))
    for name, factor in factors.items():
        out[name] = (out[name] * factor).astype(out[name].dtype)
    return out
```

```python
from contextlib import ExitStack

import concourse.bass as bass
from concourse import mybir

F32 = mybir.dt.float32
BF16 = mybir.dt.bfloat16
ALU = mybir.AluOpType
ACT = mybir.ActivationFunctionType
AX = mybir.AxisListType

P = 128
B, T, D = 2, 1024, 128
N = B * T
CH = 512
NC = N // CH
LN_EPS = 1e-5

HA = 16
QB = T // P
DEPTH, HEADS, DH, WIN = 6, 16, 64, 32
INNER = HEADS * DH
PAIRS = HEADS // 2
BLK = 64
NB = CH // BLK
KEYS = BLK + WIN
QK_SCALE = 8.0
FI = int(D * 4 * 2 / 3)
FT = -(-FI // P)
FR = FI - (FT - 1) * P
HG, DG = 4, 32
KK = P // DG
KG = DG // KK
NEG = -1e30
SS_SCALE = 2.0 ** 16
SS_EPS = 1e-24 * SS_SCALE
SS_BACK = 8 * 0.6931471805599453
ONE = 1


def pipelined(eng, per, count, lag, slot, peel_last=False):
    def run(it, first=False, end=False):
        for j in range(lag if end else per):
            def unit(k, j=j):
                back, jj = divmod(j - k, per)
                if (first and back < 0) or (end and back >= 0):
                    return None
                return it + back, jj
            slot(j, unit)
    assert lag <= per
    run(0, first=True)
    with eng.Fori(1, count - 1 if peel_last else count) as it:
        run(it)
    if peel_last:
        run(count - 1)
    run(count, end=True)


def hybrid_kernel(nc, w, c, out):
    ctx = ExitStack()
    scope = [ctx]

    def sb(name, shape, dt=F32):
        return scope[0].enter_context(nc.sbuf_tensor(name, shape, dt))

    def sem(name):
        return ctx.enter_context(nc.semaphore(name))

    with ctx:
        bank = [ctx.enter_context(nc.psum_tensor(f"bank{i}", [P, CH], F32)) for i in range(4)]
        wide = [ctx.enter_context(nc.psum_tensor(f"wide{i}", [P, 2 * CH], F32)) for i in range(2)]
        bank += [wide[0][:, 0:CH], wide[0][:, CH:2 * CH], wide[1][:, 0:CH], wide[1][:, CH:2 * CH]]
        xT = sb("xT", [P, N])
        y = sb("y", [P, N])
        ident = sb("ident", [P, P])
        identb = sb("identb", [P, P], BF16)
        jmean = sb("jmean", [P, P])
        cen = sb("cen", [P, NC, CH])
        sqr = sb("sqr", [P, NC, CH])
        rstd = sb("rstd", [P, NC, CH])

        const_ld = sem("const_ld")
        x_ld, tin_mm, tin_cp = sem("x_ld"), sem("tin_mm"), sem("tin_cp")
        mean_mm, cen_done, sqr_done, var_mm = sem("mean_mm"), sem("cen_done"), sem("sqr_done"), sem("var_mm")
        lnv_done, rstd_done, norm_done = sem("lnv_done"), sem("rstd_done"), sem("norm_done")

        def cs(k):
            return slice(k * CH, (k + 1) * CH)

        def ln_pe(pe, n, src, ready=None):
            for k in range(NC):
                if ready:
                    ready(pe, k)
                pe.matmul(bank[k][:, :], jmean[:, :], src(k), start=True, stop=True).then_inc(mean_mm, 1)
            for k in range(NC):
                pe.wait_ge(sqr_done, NC * n + k + 1)
                pe.matmul(bank[4 + k], jmean[:, :], sqr[:, k, :], start=True, stop=True).then_inc(var_mm, 1)

        def ln_act(act, n):
            act.preload_act_table_set("natural_log_exp_and_others")
            for k in range(NC):
                act.wait_ge(cen_done, NC * n + k + 1)
                act.activation(sqr[:, k, :], cen[:, k, :], ACT.Square).then_inc(sqr_done, 1)
            for k in range(NC):
                act.wait_ge(var_mm, NC * n + k + 1)
                act.activation(rstd[:, k, :], bank[4 + k], ACT.Ln, bias=ln_eps[:, 0:1]).then_inc(lnv_done, 1)
            for k in range(NC):
                act.wait_ge(lnv_done, NC * n + k + 1)
                act.activation(rstd[:, k, :], rstd[:, k, :], ACT.Exp, scale=-0.5).then_inc(rstd_done, 1)

        def ln_dve(dve, n, src, dst, gain=None):
            for k in range(NC):
                dve.wait_ge(mean_mm, NC * n + k + 1)
                dve.tensor_tensor(cen[:, k, :], src(k), bank[k][:, :], ALU.subtract).then_inc(cen_done, 1)
            for k in range(NC):
                dve.wait_ge(rstd_done, NC * n + k + 1)
                if gain is None:
                    dve.tensor_tensor(dst(k), cen[:, k, :], rstd[:, k, :], ALU.mult).then_inc(norm_done, 1)
                else:
                    dve.scalar_tensor_tensor(out=dst(k), in0=cen[:, k, :], scalar=gain, in1=rstd[:, k, :],
                                             op0=ALU.mult, op1=ALU.mult).then_inc(norm_done, 1)

        ln_eps = sb("ln_eps", [P, 1])
        ss_eps = sb("ss_eps", [P, 1])
        ss_back = sb("ss_back", [P, 1])
        eps_set = sem("eps_set")

        with ExitStack() as inner:
            scope[0] = inner
            xtok = sb("xtok", [P, N // P, D])
            with nc.Block() as block:
                @block.sync
                def _(sp):
                    for n, (dst, src) in enumerate(((ident[:, :], c["ident"]), (identb[:, :], c["identb"]),
                                                    (jmean[:, :], c["jmean"]))):
                        sp.dma_start(dst, src).then_inc(const_ld, 16)
                    sp.dma_start(xtok[:, :, :], w["L0_attn_a_x"].rearrange("b (n p) d -> p (b n) d", p=P))\
                        .then_inc(x_ld, 16)

                @block.tensor
                def _(pe):
                    pe.wait_ge(const_ld, 48)
                    pe.wait_ge(x_ld, 16)
                    for k in range(NC):
                        for i in range(4):
                            m = pe.transpose(bank[k][:, i * P:(i + 1) * P], xtok[:, 4 * k + i, :], ident[:, :])
                        m.then_inc(tin_mm, 1)

                @block.scalar
                def _(act):
                    for k in range(NC):
                        act.wait_ge(tin_mm, k + 1)
                        act.activation(xT[:, cs(k)], bank[k][:, :], ACT.Copy).then_inc(tin_cp, 1)

                @block.vector
                def _(dve):
                    dve.memset(ln_eps[:, :], LN_EPS).then_inc(eps_set, 1)
                    dve.memset(ss_eps[:, :], SS_EPS).then_inc(eps_set, 1)
                    dve.memset(ss_back[:, :], SS_BACK).then_inc(eps_set, 1)
            scope[0] = ctx

        stage_a(nc, w, c, sem, bank, wide, xT, y, ident, identb, ln_pe, ln_act, ln_dve, cs, 0)
        S = stack_semaphores(sem)
        common = (S, nc, w, c, bank, wide, xT, y, ident, identb, ln_eps, ss_eps, ss_back,
                  ln_pe, ln_act, ln_dve, norm_done, cs, cen)
        stack(0, 1, *common)
        stage_c(nc, w, c, sem, bank, wide, xT, y, ident, jmean, ln_eps, sqr, rstd, ln_pe, ln_act, ln_dve, norm_done, cs, 8)
        stack(1, 9, *common)

        out_mm, out_cp, out_st = sem("out_mm"), sem("out_cp"), sem("out_st")
        with ExitStack() as inner:
            scope[0] = inner
            otok = sb("otok", [P, N // P, D])
            with nc.Block() as block:
                @block.tensor
                def _(pe):
                    for k in range(NC):
                        for i in range(4):
                            m = pe.transpose(bank[k][:, i * P:(i + 1) * P],
                                             xT[:, (4 * k + i) * P:(4 * k + i + 1) * P], ident[:, :])
                        m.then_inc(out_mm, 1)

                @block.scalar
                def _(act):
                    for k in range(NC):
                        act.wait_ge(out_mm, k + 1)
                        act.activation(otok[:, 4 * k:4 * k + 4, :],
                                       bank[k][:, :].rearrange("p (i d) -> p i d", i=4), ACT.Copy).then_inc(out_cp, 1)

                @block.sync
                def _(sp):
                    ov = out.rearrange("b (n p) d -> p (b n) d", p=P)
                    for k in range(NC):
                        sp.wait_ge(out_cp, k + 1)
                        sp.dma_start(ov[:, 4 * k:4 * k + 4, :], otok[:, 4 * k:4 * k + 4, :]).then_inc(out_st, 16)
                    sp.wait_ge(out_st, 16 * NC)
            scope[0] = ctx


def stage_a(nc, w, c, sem, bank, wide, xT, y, ident, identb, ln_pe, ln_act, ln_dve, cs, ln_call):
    with ExitStack() as st:
        def sb(name, shape, dt=F32):
            return st.enter_context(nc.sbuf_tensor(name, shape, dt))

        wtok = sb("a_wtok", [P, 4, D])
        wT = sb("a_wT", [P, 4, D])
        bias = sb("a_bias", [P, 4])
        hmask = sb("a_hmask", [P, HA])
        cmask = sb("a_cmask", [P, HA, D])
        dmask = sb("a_dmask", [P, P], BF16)
        zero = sb("a_zero", [P, CH], BF16)
        qT = sb("a_qT", [P, N])
        kT = sb("a_kT", [P, N])
        v = sb("a_v", [P, N // P, D])
        qm = sb("a_qm", [P, T])
        vm = sb("a_vm", [P, QB, D])
        prob = sb("a_prob", [P, 4, T])
        pT = sb("a_pT", [P, 2, QB, P])
        nmax = sb("a_nmax", [P, 4])
        rsum = sb("a_rsum", [P, 4])
        rinv = sb("a_rinv", [P, 4])
        oT = sb("a_oT", [P, T])
        a_ld = sem("a_ld")
        wt_mm, wt_cp, zero_set = sem("a_wt_mm"), sem("a_wt_cp"), sem("a_zero_set")
        pr_mm, pr_cp = sem("a_pr_mm"), sem("a_pr_cp")

        norm_done = sem("a_normed")

        def hT(k):
            return y[:, cs(k)]

        with nc.Block() as block:
            @block.sync
            def _(sp):
                for i, nm in enumerate("qkvo"):
                    sp.dma_start(wtok[:, i, :], w[f"L0_attn_a_W{nm}_w"]).then_inc(a_ld, 16)
                    sp.dma_start(bias[:, i:i + 1], w[f"L0_attn_a_W{nm}_b"].rearrange("(p a) -> p a", a=1))\
                        .then_inc(a_ld, 16)
                for dst, src in ((hmask[:, :], c["a_hmask"]), (cmask[:, :, :], c["a_cmask"]), (dmask[:, :], c["a_dmask"])):
                    sp.dma_start(dst, src).then_inc(a_ld, 16)

            @block.tensor
            def _(pe):
                ln_pe(pe, ln_call, lambda k: xT[:, cs(k)])
                pe.wait_ge(a_ld, 16 * 11)
                pe.wait_ge(norm_done, 1)
                for i in range(4):
                    m = pe.transpose(bank[0][:, i * P:(i + 1) * P], wtok[:, i, :], ident[:, :])
                m.then_inc(wt_mm, 1)
                pe.wait_ge(wt_cp, 1)
                for k in range(NC):
                    for i in range(3):
                        n = 3 * k + i
                        o = bank[1 + n % 6] if n % 6 > 2 else bank[1 + n % 6][:, :]
                        if n >= 6:
                            pe.wait_ge(pr_cp, n - 5)
                        if i < 2:
                            m = pe.matmul(o, wT[:, i, :], hT(k), start=True, stop=True)
                        else:
                            for t in range(4):
                                m = pe.matmul(o[:, t * P:(t + 1) * P], y[:, (4 * k + t) * P:(4 * k + t + 1) * P],
                                              wT[:, 2, :], start=(t == 0), stop=(t == 3), skip_group_check=True)
                        m.then_inc(pr_mm, 1)

            @block.scalar
            def _(act):
                ln_act(act, ln_call)
                act.wait_ge(wt_mm, 1)
                act.activation(wT[:, :, :], bank[0][:, :].rearrange("p (i d) -> p i d", i=4), ACT.Copy).then_inc(wt_cp, 1)
                for n in range(3 * NC):
                    k, i = divmod(n, 3)
                    src = bank[1 + n % 6] if n % 6 > 2 else bank[1 + n % 6][:, :]
                    act.wait_ge(pr_mm, n + 1)
                    if i < 2:
                        act.activation((qT, kT)[i][:, cs(k)], src, ACT.Identity, bias=bias[:, i:i + 1]).then_inc(pr_cp, 1)
                    else:
                        act.activation(v[:, 4 * k:4 * k + 4, :], src.rearrange("p (t d) -> p t d", t=4), ACT.Copy)\
                            .then_inc(pr_cp, 1)

            @block.vector
            def _(dve):
                dve.memset(zero[:, :], 0.0).then_inc(zero_set, 1)
                ln_dve(dve, ln_call, lambda k: xT[:, cs(k)], hT)
                dve.drain().then_inc(norm_done, 1)

        s_mm, smax_done, exp_done = sem("a_s_mm"), sem("a_smax_done"), sem("a_exp_done")
        rinv_done, pn_done = sem("a_rinv_done"), sem("a_pn_done")
        t_mm = [sem("a_t_mm0"), sem("a_t_mm1")]
        pt_cp = [sem("a_pt_cp0"), sem("a_pt_cp1")]
        pv_mm = sem("a_pv_mm")
        qm_done, vm_done = sem("a_qm_done"), sem("a_vm_done")
        o_cp, wo_mm, res_done = sem("a_o_cp"), sem("a_wo_mm"), sem("a_res_done")
        units = HA * QB
        LAG = 2
        SC, PR = 2, 4
        scores = [wide[0], wide[1]]
        turned = [bank[0], bank[1]]
        oacc = [bank[2], bank[3]]

        def at(b, u):
            return units * b + QB * u[0] + u[1], HA * b + u[0], u[1]

        def grp(a, n, g, i):
            return n + 1 if a == 0 else 4 * g + i - 3

        with nc.Block() as block:
            @block.tensor
            def _(pe):
                for b in range(B):
                    if b:
                        pe.wait_ge(o_cp, 2 * b)
                        pe.wait_ge(res_done, 2 * b)
                    for a in range(2):
                        pe.matmul(oacc[a][:, :], zero[:, 0:P], zero[:, :], start=True, stop=False, skip_group_check=True)

                    def slot(j, unit, b=b):
                        u = unit(0)
                        if u:
                            n, g, i = at(b, u)
                            s = scores[i % SC]
                            if i == 0:
                                pe.wait_ge(qm_done, g + 1)
                            pe.wait_ge(exp_done, n + 1)
                            for a in range((i + 4) // 4):
                                e = min(CH * (a + 1), P * (i + 1))
                                pe.matmul(s[:, CH * a:e], qm[:, i * P:(i + 1) * P], kT[:, b * T + CH * a:b * T + e],
                                          start=True, stop=False, skip_group_check=True)
                            pe.matmul(s[:, i * P:(i + 1) * P], identb[:, :], dmask[:, :],
                                      start=False, stop=True, skip_group_check=True).then_inc(s_mm, 1)
                        u = unit(LAG)
                        if u:
                            n, g, i = at(b, u)
                            if i == 0:
                                pe.wait_ge(vm_done, g + 1)
                            pe.wait_ge(pn_done, n + 1)
                            for a in range((i + 4) // 4):
                                pe.wait_ge(pt_cp[a], grp(a, n, g, i) - 1)
                                for kb in range(4 * a, min(4 * a + 4, i + 1)):
                                    m = pe.transpose(turned[a][:, (kb % 4) * P:(kb % 4 + 1) * P],
                                                     prob[:, i % PR, kb * P:(kb + 1) * P], ident[:, :])
                                m.then_inc(t_mm[a], 1)
                            for kb in range(i + 1):
                                if kb % 4 == 0:
                                    pe.wait_ge(pt_cp[kb // 4], grp(kb // 4, n, g, i))
                                m = pe.matmul(oacc[i // 4][:, (i % 4) * P:(i % 4 + 1) * P], vm[:, kb, :],
                                              pT[:, i % 2, kb, :], start=False, stop=False, skip_group_check=True)
                            m.then_inc(pv_mm, 1)
                    pipelined(pe, QB, HA, LAG, slot)
                    for a in range(2):
                        pe.wait_ge(o_cp, 2 * b + a + 1)
                        pe.matmul(scores[0][:, a * CH:(a + 1) * CH], wT[:, 3, :], oT[:, a * CH:(a + 1) * CH],
                                  start=True, stop=True).then_inc(wo_mm, 1)

            @block.scalar
            def _(act):
                act.sem_inc(exp_done, SC)
                for b in range(B):
                    def slot(j, unit, b=b):
                        u = unit(0)
                        if u:
                            n, g, i = at(b, u)
                            act.wait_ge(smax_done, n + 1)
                            act.wait_ge(pv_mm, n + 1)
                            e = P * (i + 1)
                            act.activation(prob[:, i % PR, 0:e], scores[i % SC][:, 0:e], ACT.Exp, bias=nmax[:, i % 4:i % 4 + 1],
                                           accum_out=rsum[:, i % 4:i % 4 + 1]).then_inc(exp_done, 1)
                        u = unit(LAG)
                        if u:
                            n, g, i = at(b, u)
                            act.wait_ge(pv_mm, n + 1 + PR - 2)
                            for a in range((i + 4) // 4):
                                k = min(4, i + 1 - 4 * a)
                                act.wait_ge(t_mm[a], grp(a, n, g, i))
                                act.activation(pT[:, i % 2, 4 * a:4 * a + k, :],
                                               turned[a][:, 0:k * P].rearrange("p (k q) -> p k q", k=k), ACT.Copy)\
                                    .then_inc(pt_cp[a], 1)
                    pipelined(act, QB, HA, LAG, slot)
                    act.wait_ge(pv_mm, units * (b + 1) + PR)
                    if b:
                        act.wait_ge(wo_mm, 2 * b)
                    for a in range(2):
                        act.activation(oT[:, a * CH:(a + 1) * CH], oacc[a][:, :], ACT.Identity, bias=bias[:, 2:3])\
                            .then_inc(o_cp, 1)

            @block.gpsimd
            def _(pool):
                pool.sem_inc(pv_mm, PR)
                for b in range(B):
                    with pool.Fori(0, HA) as h:
                        pool.wait_ge(pv_mm, units * b + QB * h + PR)
                        pool.tensor_tensor(vm[:, :, :], v[:, QB * b:QB * b + QB, :],
                                           cmask[:, bass.ds(h, 1), :].broadcast_to([P, QB, D]), ALU.mult).then_inc(vm_done, 1)

            @block.vector
            def _(dve):
                for b in range(B):
                    def slot(j, unit, b=b):
                        u = unit(0)
                        if u:
                            n, g, i = at(b, u)
                            if i == 0:
                                dve.wait_ge(s_mm, n)
                                dve.tensor_scalar(qm[:, :], qT[:, b * T:(b + 1) * T], hmask[:, bass.ds(u[0], 1)], None, ALU.mult)\
                                    .then_inc(qm_done, 1)
                            dve.wait_ge(s_mm, n + 1)
                            dve.wait_ge(exp_done, n + 1)
                            dve.tensor_reduce(nmax[:, i % 4:i % 4 + 1], scores[i % SC][:, 0:P * (i + 1)], AX.X, ALU.max,
                                              negate=True).then_inc(smax_done, 1)
                        u = unit(1)
                        if u:
                            n, g, i = at(b, u)
                            dve.wait_ge(exp_done, n + 1 + SC)
                            dve.reciprocal(rinv[:, i % 4:i % 4 + 1], rsum[:, i % 4:i % 4 + 1]).then_inc(rinv_done, 1)
                            dve.wait_ge(rinv_done, n + 1)
                            dve.tensor_scalar(prob[:, i % PR, 0:P * (i + 1)], prob[:, i % PR, 0:P * (i + 1)],
                                              rinv[:, i % 4:i % 4 + 1], None, ALU.mult).then_inc(pn_done, 1)
                    pipelined(dve, QB, HA, 1, slot)
                    for a in range(2):
                        dve.wait_ge(wo_mm, 2 * b + a + 1)
                        xs = xT[:, b * T + a * CH:b * T + (a + 1) * CH]
                        dve.scalar_tensor_tensor(out=xs, in0=scores[0][:, a * CH:(a + 1) * CH], scalar=bias[:, 3:4], in1=xs,
                                                 op0=ALU.add, op1=ALU.add).then_inc(res_done, 1)


def stack_semaphores(sem):
    names = """ld const_ld zeroed wst_ld wqkv_ready wo_ready ffw_ld q_mm k_mm ssq_mm ssk_mm va_mm vb_mm
            s_mm t_mm pv_mm wo_mm sqq_done sqk_done rlq_done rlk_done rq_done rk_done va_cp vb_cp exp_done
            pt_cp o_cp pq_done pk_done swap_ld addq_done addk_done qn_done kn_done smax_done ssub_done
            ssum_done rinv_done pn_done y_add y_start shift_done a_mm g_mm gelu_done h_done out_mm y_done
            bias_done x_done"""
    return {n: sem("b_" + n) for n in names.split()}


def stack(rep, ln_call, S, nc, w, c, bank, wide, xT, y, ident, identb, ln_eps, ss_eps, ss_back,
          ln_pe, ln_act, ln_dve, norm_done, cs, cen):
    with ExitStack() as st:
        def sb(name, shape, dt=F32):
            return st.enter_context(nc.sbuf_tensor(f"b{rep}_{name}", shape, dt))

        PAD = BLK
        xs = sb("xs", [P, PAD + N])
        rot = sb("rot", [P, 4, T])
        band = sb("band", [P, 2, 4 * KEYS], BF16)
        same = sb("same", [P, P])
        wst = sb("wst", [P, 4, P])
        wqkv = sb("wqkv", [P, 3, P])
        wo = sb("wo", [P, P])
        qks = sb("qks", [P, 2])
        lng = sb("lng", [P, 2])
        w1 = sb("w1", [P, 2, FT * P])
        w2 = sb("w2", [P, FT, P])
        b1 = sb("b1", [P, 2, FT])
        b2 = sb("b2", [P, 1])
        sq = sb("sq", [P, 2, CH])
        rr = sb("rr", [P, 2, 2, CH])
        prc = sb("prc", [P, 2, 2, CH])
        prs = sb("prs", [P, 2, 2, CH])
        sws = sb("sws", [P, 2, 2, CH])
        qd = sb("qd", [P, 2, NB, 2, BLK])
        kr = sb("kr", [P, PAD + T])
        vb = sb("vb", [P, 4, 2, 4, P])
        prob = sb("prob", [P, 4, NB, P])
        smx = sb("smx", [P, 2, NB])
        ssm = sb("ssm", [P, 2, NB])
        rinv = sb("rinv", [P, 2, NB])
        pT = sb("pT", [P, 2, 4, P])
        oT = sb("oT", [P, 2, NB, BLK])
        gel = sb("gel", [P, FT, CH])
        hid = sb("hid", [P, 2, FT, CH])

        L0 = DEPTH * rep
        U0 = 32 * L0

        def um(u, l):
            return 32 * l + 4 * u[0] + u[1], u[1]

        def at_bank(i):
            return bank[i] if i >= 4 else bank[i][:, :]

        with nc.Block() as block:
            @block.sync
            def _(sp):
                for dst, src in ((rot[:, :, :], c["rot"]), (band[:, :, :], c["band"]), (same[:, :], c["same_head"])):
                    sp.dma_start(dst, src).then_inc(S["const_ld"], 16)
                with sp.Fori(L0, L0 + DEPTH) as l:
                    li = l - L0

                    def pair_weights(p, sp=sp, l=l, li=li):
                        sp.wait_ge(S["wqkv_ready"], ONE + PAIRS * l + p)
                        sp.wait_ge(S["wo_ready"], ONE + PAIRS * l + p)
                        sp.wait_ge(S["zeroed"], ONE + 9 * (rep + 1))
                        wq = w["L0_ffn_Wqkv"][li, :, :].rearrange("d (i q f) -> d i q f", i=3, f=P)
                        sp.dma_start(wst[:, 0:3, :], wq[:, :, p, :]).then_inc(S["wst_ld"], 16)
                        sp.dma_start(wst[:, 3, :], w["L0_ffn_Wo"][li, bass.ts(p, P), :]).then_inc(S["wst_ld"], 16)
                    pair_weights(0)
                    sp.wait_ge(S["y_done"], ONE + NC * l)
                    sp.wait_ge(S["zeroed"], ONE + 9 * (rep + 1))
                    for i, nm in enumerate(("L0_ffn_q_scale", "L0_ffn_k_scale")):
                        for h in range(2):
                            sp.dma_start(qks[h * DH:(h + 1) * DH, i:i + 1], w[nm][li, :].rearrange("(p a) -> p a", a=1))\
                                .then_inc(S["ld"], 16)
                    f = "L0_ffn_"
                    for a in range(2):
                        sp.dma_start(w1[:, a, 0:FI], w[f + "W1"][li, :, a * FI:(a + 1) * FI]).then_inc(S["ffw_ld"], 16)
                        for i in range(FT):
                            r = P if i < FT - 1 else FR
                            sp.dma_start(b1[0:r, a, i:i + 1], w[f + "b1"][li, a * FI + i * P:a * FI + i * P + r]
                                         .rearrange("(p a) -> p a", a=1)).then_inc(S["ffw_ld"], 16)
                    sp.dma_start(w2[:, 0:FT - 1, :], w[f + "W2"][li, 0:(FT - 1) * P, :].rearrange("(i p) d -> p i d", p=P))\
                        .then_inc(S["ffw_ld"], 16)
                    sp.dma_start(w2[0:FR, FT - 1, :], w[f + "W2"][li, (FT - 1) * P:FI, :]).then_inc(S["ffw_ld"], 16)
                    for dst, nm in ((lng[:, 0:1], "ln_g"), (lng[:, 1:2], "ln_b"), (b2[:, 0:1], "b2")):
                        sp.dma_start(dst, w[f + nm][li, :].rearrange("(p a) -> p a", a=1)).then_inc(S["ffw_ld"], 16)

                    def slot(j, unit, sp=sp, l=l):
                        u = unit(0)
                        if u:
                            U, k = um(u, l)
                            sp.wait_ge(S["pk_done"], ONE + U + 1)
                            for h in range(4):
                                o = h ^ 1
                                sp.dma_start(sws[32 * o:32 * o + 32, k % 2, :, :], prs[32 * h:32 * h + 32, k % 2, :, :])\
                                    .then_inc(S["swap_ld"], 16)
                    for j in range(4):
                        slot(j, lambda k, j=j: (0, j))
                    with sp.Fori(1, PAIRS) as p:
                        pair_weights(p)
                        for j in range(4):
                            slot(j, lambda k, j=j: (p, j))

            @block.gpsimd
            def _(pool):
                if rep == 0:
                    for s in S.values():
                        pool.sem_inc(s, ONE)
                for t in (w1[:, :, :], w2[:, :, :], b1[:, :, :], qd[:, :, :, :, :], kr[:, 0:PAD], xs[:, 0:PAD],
                          prob[:, :, :, 0:P - KEYS]):
                    pool.memset(t, 0.0).then_inc(S["zeroed"], 1)
                pool.wait_ge(S["zeroed"], ONE + 9 * rep + 7)
                for b in range(B):
                    pool.memset(xs[BLK:P, PAD + b * T:PAD + b * T + 1], 0.0).then_inc(S["zeroed"], 1)
                with pool.Fori(L0, L0 + DEPTH) as l:
                    def slot(j, unit, pool=pool, l=l):
                        u = unit(2)
                        if u:
                            U, k = um(u, l)
                            pool.wait_ge(S["rinv_done"], ONE + U + 1)
                            pool.tensor_tensor(prob[:, k, :, P - KEYS:P], prob[:, k, :, P - KEYS:P],
                                               rinv[:, k % 2, :].rearrange("p (b a) -> p b a", a=1).broadcast_to([P, NB, KEYS]),
                                               ALU.mult).then_inc(S["pn_done"], 1)
                        u = unit(0)
                        if u:
                            U, k = um(u, l)
                            pool.wait_ge(S["swap_ld"], ONE + 64 * (U + 1))
                            for i, nm in enumerate(("addq_done", "addk_done")):
                                pool.tensor_tensor(prc[:, k % 2, i, :], prc[:, k % 2, i, :], sws[:, k % 2, i, :], ALU.add)\
                                    .then_inc(S[nm], 1)
                    pipelined(pool, 4, PAIRS, 3, slot)

            @block.tensor
            def _(pe):
                pe.wait_ge(S["const_ld"], ONE + 48 * (rep + 1))
                ln_pe(pe, ln_call, lambda k: xT[:, cs(k)])
                with pe.Fori(L0, L0 + DEPTH) as l:
                    def slot(j, unit, pe=pe, l=l):
                        a, b, d = unit(0), unit(1), unit(3)
                        if a:
                            U, k = um(a, l)
                            X = xs[:, PAD + k * CH:PAD + (k + 1) * CH]
                            if j == 0:
                                pe.wait_ge(S["wqkv_ready"], ONE + PAIRS * l + a[0] + 1)
                            pe.wait_ge(S["va_cp"], ONE + U)
                            pe.matmul(bank[0][:, :], wqkv[:, 0, :], X, start=True, stop=True).then_inc(S["q_mm"], 1)
                        if d:
                            UD, kd = um(d, l)
                            turn(pe, UD, kd, 0)
                        if a:
                            pe.wait_ge(S["vb_cp"], ONE + U)
                            pe.matmul(bank[1][:, :], wqkv[:, 1, :], X, start=True, stop=True).then_inc(S["k_mm"], 1)
                        if d:
                            values(pe, UD, kd, 0)
                        if a:
                            pe.wait_ge(S["sqq_done"], ONE + U + 1)
                            pe.wait_ge(S["y_add"], ONE + UD if d else 32 * l)
                            pe.matmul(bank[2][:, :], same[:, :], sq[:, 0, :], start=True, stop=True).then_inc(S["ssq_mm"], 1)
                        if d:
                            turn(pe, UD, kd, 1)
                        if b:
                            UB, kb = um(b, l)
                            first = kb % 2 == 0
                            pe.wait_ge(S["kn_done"], ONE + UB + 1)
                            pe.wait_ge(S["ssub_done"], ONE + UB)
                            for h in range(2):
                                s = wide[0][:, h * CH:h * CH + 4 * KEYS]
                                pe.matmul(s, identb[:, :], band[:, 0 if first and h == 0 else 1, :],
                                          start=True, stop=False, skip_group_check=True)
                                for i in range(4):
                                    n = 4 * h + i
                                    at = PAD + (kb % 2) * CH + n * BLK - WIN
                                    m = pe.matmul(s[:, i * KEYS:(i + 1) * KEYS], qd[:, kb % 2, n, :, :]
                                                  .rearrange("p h q -> p (h q)"), kr[:, at:at + KEYS],
                                                  start=False, stop=(i == 3), skip_group_check=True)
                            m.then_inc(S["s_mm"], 1)
                        if d:
                            values(pe, UD, kd, 1)
                        if a:
                            pe.wait_ge(S["sqk_done"], ONE + U + 1)
                            pe.wait_ge(S["rlk_done"], ONE + U)
                            pe.matmul(bank[3][:, :], same[:, :], sq[:, 1, :], start=True, stop=True).then_inc(S["ssk_mm"], 1)
                            for o, free, nm, off in ((0, "pq_done", "va_mm", 0), (1, "pk_done", "vb_mm", -BLK)):
                                pe.wait_ge(S[free], ONE + U + 1)
                                for t in range(4):
                                    at = PAD + k * CH + t * P + off
                                    m = pe.matmul(bank[o][:, t * P:(t + 1) * P], xs[:, at:at + P], wqkv[:, 2, :],
                                                  start=(t == 0), stop=(t == 3), skip_group_check=True)
                                m.then_inc(S[nm], 1)
                        if d:
                            if kd == 0:
                                pe.wait_ge(S["wo_ready"], ONE + PAIRS * l + d[0] + 1)
                            pe.wait_ge(S["o_cp"], ONE + 4 * UD + 4)
                            if a:
                                pe.wait_ge(S["rlq_done"], ONE + U + 1)
                            else:
                                pe.wait_ge(S["rlq_done"], ONE + 32 * l + 32)
                                pe.wait_ge(S["y_add"], ONE + UD)
                            pe.matmul(bank[2][:, :], wo[:, :], oT[:, kd % 2, :, :].rearrange("p b q -> p (b q)"),
                                      start=True, stop=True).then_inc(S["wo_mm"], 1)

                    def turn(pe, UD, kd, h):
                        if h == 0:
                            pe.wait_ge(S["pn_done"], ONE + UD + 1)
                        pe.wait_ge(S["pt_cp"], ONE + 2 * UD + h)
                        for i in range(4):
                            m = pe.transpose(bank[6][:, i * P:(i + 1) * P], prob[:, kd, 4 * h + i, :], ident[:, :])
                        m.then_inc(S["t_mm"], 1)

                    def values(pe, UD, kd, h):
                        pe.wait_ge(S["pt_cp"], ONE + 2 * UD + h + 1)
                        pe.wait_ge(S["o_cp"], ONE + 4 * UD + 2 * h)
                        for i in range(4):
                            n = 4 * h + i
                            v = vb[:, kd, 1 - n % 2, n // 2, :]
                            m = pe.matmul(bank[7][:, i * P:(i + 1) * P], v, pT[:, h, i, :],
                                          start=(i == 0), stop=(i == 3), skip_group_check=True)
                        m.then_inc(S["pv_mm"], 1)

                    pe.wait_ge(S["shift_done"], ONE + 4 * l + 2)
                    pipelined(pe, 4, PAIRS, 3, slot)


                    pe.wait_ge(S["shift_done"], ONE + 4 * l + 4)
                    for name, count in (("va_cp", 32), ("vb_cp", 32), ("y_add", 32), ("rlk_done", 32),
                                        ("ssub_done", 32), ("pt_cp", 64), ("o_cp", 128)):
                        pe.wait_ge(S[name], ONE + count * (l + 1))
                    ln_pe(pe, ln_call + 1 + (l - L0), lambda k: xs[:, PAD + k * CH:PAD + (k + 1) * CH])
                    pe.wait_ge(S["ffw_ld"], ONE + 208 * (l + 1))

                    def up(k, pe=pe, l=l):
                        pe.wait_ge(S["bias_done"], ONE + NC * l + k + 1)
                        for i in range(FT):
                            if k:
                                pe.wait_ge(S["h_done"], ONE + FT * (NC * l + k - 1) + i + 1)
                            for a, nm in enumerate(("a_mm", "g_mm")):
                                pe.matmul(at_bank(2 * i + a), w1[:, a, i * P:(i + 1) * P], cen[:, k, :],
                                          start=True, stop=True).then_inc(S[nm], 1)
                    up(0)
                    for k in range(NC):
                        if k + 1 < NC:
                            up(k + 1)
                        pe.wait_ge(S["h_done"], ONE + FT * (NC * l + k + 1))
                        if k >= 2:
                            pe.wait_ge(S["y_done"], ONE + NC * l + k - 1)
                        for i in range(FT):
                            m = pe.matmul(bank[6 + k % 2], w2[:, i, :], hid[:, k % 2, i, :], start=(i == 0), stop=(i == FT - 1))
                        m.then_inc(S["out_mm"], 1)

            @block.scalar
            def _(act):
                ln_act(act, ln_call)
                with act.Fori(L0, L0 + DEPTH) as l:
                    act.preload_act_table_set("natural_log_exp_and_others")
                    def slot(j, unit, act=act, l=l):
                        a, b, d = unit(0), unit(1), unit(3)

                        def turned(h):
                            act.wait_ge(S["t_mm"], ONE + 2 * UD + h + 1)
                            act.activation(pT[:, h, :, :], bank[6].rearrange("p (i q) -> p i q", i=4), ACT.Copy)\
                                .then_inc(S["pt_cp"], 1)

                        def outputs(h):
                            act.wait_ge(S["pv_mm"], ONE + 2 * UD + h + 1)
                            o = bank[7].rearrange("p (i h q) -> p i h q", i=4, h=2)
                            for e in range(2):
                                act.activation(oT[e * DH:(e + 1) * DH, kd % 2, 4 * h:4 * h + 4, :],
                                               o[e * DH:(e + 1) * DH, :, e, :], ACT.Copy).then_inc(S["o_cp"], 1)

                        def inverse_norm(i, mm, ln, done):
                            act.wait_ge(S[mm], ONE + U + 1)
                            act.activation(rr[:, k % 2, i, :], bank[2 + i][:, :], ACT.Ln, bias=ss_eps[:, 0:1], scale=SS_SCALE)\
                                .then_inc(S[ln], 1)
                            act.wait_ge(S[ln], ONE + U + 1)
                            act.activation(rr[:, k % 2, i, :], rr[:, k % 2, i, :], ACT.Exp, bias=ss_back[:, 0:1], scale=-0.5)\
                                .then_inc(S[done], 1)
                        if a and j == 0:
                            g = PAIRS * l + a[0]
                            act.wait_ge(S["wst_ld"], ONE + 32 * (g + 1))
                            act.wait_ge(S["vb_mm"], ONE + 4 * g)
                            act.activation(wqkv[:, :, :], wst[:, 0:3, :], ACT.Copy).then_inc(S["wqkv_ready"], 1)
                        if a and j == 3:
                            g = PAIRS * l + a[0]
                            act.wait_ge(S["wo_mm"], ONE + 4 * g)
                            act.activation(wo[:, :], wst[:, 3, :], ACT.Copy).then_inc(S["wo_ready"], 1)
                        if a:
                            U, k = um(a, l)
                            act.wait_ge(S["q_mm"], ONE + U + 1)
                            act.activation(sq[:, 0, :], bank[0][:, :], ACT.Square).then_inc(S["sqq_done"], 1)
                        if d:
                            UD, kd = um(d, l)
                            turned(0)
                        if a:
                            act.wait_ge(S["k_mm"], ONE + U + 1)
                            act.activation(sq[:, 1, :], bank[1][:, :], ACT.Square).then_inc(S["sqk_done"], 1)
                        if d:
                            outputs(0)
                        if a:
                            inverse_norm(0, "ssq_mm", "rlq_done", "rq_done")
                        if d:
                            turned(1)
                            outputs(1)
                        if b:
                            UB, kb = um(b, l)
                            act.wait_ge(S["ssub_done"], ONE + UB + 1)
                            act.activation(prob[:, kb, :, P - KEYS:P], prob[:, kb, :, P - KEYS:P], ACT.Exp, scale=QK_SCALE)\
                                .then_inc(S["exp_done"], 1)
                        if a:
                            inverse_norm(1, "ssk_mm", "rlk_done", "rk_done")
                            for o, mm, cp in ((0, "va_mm", "va_cp"), (1, "vb_mm", "vb_cp")):
                                act.wait_ge(S[mm], ONE + U + 1)
                                act.activation(vb[:, k, o, :, :], bank[o][:, :].rearrange("p (t d) -> p t d", t=4), ACT.Copy)\
                                    .then_inc(S[cp], 1)
                    pipelined(act, 4, PAIRS, 3, slot)
                    ln_act(act, ln_call + 1 + (l - L0))
                    for k in range(NC):
                        act.wait_ge(norm_done, NC * (ln_call + 1 + (l - L0)) + k + 1)
                        act.activation(cen[:, k, :], cen[:, k, :], ACT.Identity, bias=lng[:, 1:2])\
                            .then_inc(S["bias_done"], 1)
                    for k in range(NC):
                        for i in range(FT):
                            n = FT * (NC * l + k) + i
                            act.wait_ge(S["g_mm"], ONE + n + 1)
                            if k:
                                act.wait_ge(S["h_done"], ONE + n - FT + 1)
                            act.activation(gel[:, i, :], at_bank(2 * i + 1), ACT.Gelu, bias=b1[:, 1, i:i + 1])\
                                .then_inc(S["gelu_done"], 1)

            @block.vector
            def _(dve):
                dve.wait_ge(S["zeroed"], ONE + 9 * (rep + 1))
                dve.wait_ge(S["const_ld"], ONE + 48 * (rep + 1))
                ln_dve(dve, ln_call, lambda k: xT[:, cs(k)], lambda k: y[:, cs(k)])
                dve.wait_ge(norm_done, NC * (ln_call + 1))

                def shift():
                    dve.tensor_copy(xs[0:BLK, PAD:PAD + N], y[0:BLK, :]).then_inc(S["shift_done"], 1)
                    src = y[BLK:P, :].rearrange("p (b t) -> p b t", b=B)
                    dst = xs[BLK:P, PAD:PAD + N].rearrange("p (b t) -> p b t", b=B)
                    dve.tensor_copy(dst[:, :, 1:T], src[:, :, 0:T - 1]).then_inc(S["shift_done"], 1)

                with dve.Fori(L0, L0 + DEPTH) as l:
                    dve.wait_ge(S["y_done"], ONE + NC * l)
                    shift()
                    dve.wait_ge(S["ld"], ONE + 64 * (l + 1))

                    def slot(j, unit, dve=dve, l=l):
                        a, b, c_, d = unit(0), unit(1), unit(2), unit(3)
                        if c_:
                            UC, kc = um(c_, l)
                            dve.wait_ge(S["exp_done"], ONE + UC + 1)
                            dve.tensor_reduce(ssm[:, kc % 2, :], prob[:, kc, :, P - KEYS:P], AX.X, ALU.add)\
                                .then_inc(S["ssum_done"], 1)
                            dve.wait_ge(S["ssum_done"], ONE + UC + 1)
                            dve.reciprocal(rinv[:, kc % 2, :], ssm[:, kc % 2, :]).then_inc(S["rinv_done"], 1)
                        if b:
                            UB, kb = um(b, l)
                            dve.wait_ge(S["addq_done"], ONE + UB + 1)
                            dve.wait_ge(S["rq_done"], ONE + UB + 1)
                            for h in range(2):
                                hs = slice(h * DH, (h + 1) * DH)
                                dve.tensor_tensor(qd[hs, kb % 2, :, h, :],
                                                  prc[hs, kb % 2, 0, :].rearrange("p (n q) -> p n q", n=NB),
                                                  rr[hs, kb % 2, 0, :].rearrange("p (n q) -> p n q", n=NB), ALU.mult)\
                                    .then_inc(S["qn_done"], 1)
                            dve.wait_ge(S["addk_done"], ONE + UB + 1)
                            dve.wait_ge(S["rk_done"], ONE + UB + 1)
                            at = PAD + (kb % 2) * CH
                            dve.tensor_tensor(kr[:, at:at + CH], prc[:, kb % 2, 1, :], rr[:, kb % 2, 1, :], ALU.mult)\
                                .then_inc(S["kn_done"], 1)
                        if a:
                            U, k = um(a, l)
                            t = slice((k % 2) * CH, (k % 2 + 1) * CH)
                            for i, sqd, done in ((0, "sqq_done", "pq_done"), (1, "sqk_done", "pk_done")):
                                dve.wait_ge(S[sqd], ONE + U + 1)
                                for o, r in ((prc, 0), (prs, 1)):
                                    m = dve.scalar_tensor_tensor(out=o[:, k % 2, i, :], in0=bank[i][:, :], scalar=qks[:, i:i + 1],
                                                                 in1=rot[:, 2 * i + r, t], op0=ALU.mult, op1=ALU.mult)
                                m.then_inc(S[done], 1)
                        if b:
                            sc = wide[0][:, :].rearrange("p (h c) -> p h c", h=2)[:, :, 0:4 * KEYS]\
                                .rearrange("p h (i k) -> p h i k", k=KEYS)
                            dve.wait_ge(S["s_mm"], ONE + UB + 1)
                            dve.tensor_reduce(smx[:, kb % 2, :], sc, AX.X, ALU.max).then_inc(S["smax_done"], 1)
                            dve.wait_ge(S["smax_done"], ONE + UB + 1)
                            dve.tensor_tensor(prob[:, kb, :, P - KEYS:P].rearrange("p (h i) k -> p h i k", h=2), sc,
                                              smx[:, kb % 2, :].rearrange("p (h i a) -> p h i a", h=2, a=1)
                                              .broadcast_to([P, 2, 4, KEYS]), ALU.subtract).then_inc(S["ssub_done"], 1)
                        if d:
                            UD, kd = um(d, l)
                            dve.wait_ge(S["wo_mm"], ONE + UD + 1)
                            dve.tensor_tensor(y[:, cs(kd)], bank[2][:, :], y[:, cs(kd)], ALU.add).then_inc(S["y_add"], 1)
                    pipelined(dve, 4, PAIRS, 3, slot)
                    dve.wait_ge(S["y_add"], ONE + 32 * (l + 1))
                    shift()
                    dve.wait_ge(S["shift_done"], ONE + 4 * l + 4)
                    dve.wait_ge(S["ffw_ld"], ONE + 208 * (l + 1))
                    ln_dve(dve, ln_call + 1 + (l - L0), lambda k: xs[:, PAD + k * CH:PAD + (k + 1) * CH],
                           lambda k: cen[:, k, :], gain=lng[:, 0:1])

                    def hidden(k, dve=dve, l=l):
                        for i in range(FT):
                            n = FT * (NC * l + k) + i
                            dve.wait_ge(S["a_mm"], ONE + n + 1)
                            dve.wait_ge(S["gelu_done"], ONE + n + 1)
                            if k >= 2:
                                dve.wait_ge(S["out_mm"], ONE + NC * l + k - 1)
                            dve.scalar_tensor_tensor(out=hid[:, k % 2, i, :], in0=at_bank(2 * i), scalar=b1[:, 0, i:i + 1],
                                                     in1=gel[:, i, :], op0=ALU.add, op1=ALU.mult).then_inc(S["h_done"], 1)
                    hidden(0)
                    for k in range(NC):
                        if k + 1 < NC:
                            hidden(k + 1)
                        dve.wait_ge(S["out_mm"], ONE + NC * l + k + 1)
                        dve.scalar_tensor_tensor(out=y[:, cs(k)], in0=bank[6 + k % 2], scalar=b2[:, 0:1], in1=y[:, cs(k)],
                                                 op0=ALU.add, op1=ALU.add).then_inc(S["y_done"], 1)
                dve.wait_ge(S["y_done"], ONE + NC * (L0 + DEPTH))
                for k in range(NC):
                    dve.tensor_tensor(xT[:, cs(k)], xT[:, cs(k)], y[:, cs(k)], ALU.add).then_inc(S["x_done"], 1)


def stage_c(nc, w, c, sem, bank, wide, xT, y, ident, jmean, ln_eps, sqr, rstd, ln_pe, ln_act, ln_dve, norm_done, cs, ln_call):
    with ExitStack() as st:
        def sb(name, shape, dt=F32):
            return st.enter_context(nc.sbuf_tensor("c_" + name, shape, dt))

        names = ["w_q", "w_k", "w_v", "w_f", "w_o"]
        wtok = sb("wtok", [P, 5, D])
        wT = sb("wT", [P, 5, D])
        gains = sb("gains", [P, 2])
        hmask = sb("hmask", [P, HG])
        pick = sb("pick", [P, KG, P])
        put = sb("put", [P, KG, P])
        spread = sb("spread", [P, P])
        qkv = sb("qkv", [P, 3, N])
        f = sb("f", [P, N])
        e = sb("e", [P, N])
        s = sb("s", [P, N])
        oT = sb("oT", [P, N])
        own = sb("own", [P, 4, T])
        srep = sb("srep", [P, T])
        lrep = sb("lrep", [P, T])
        inp = sb("inp", [P, 2, T])
        stt = sb("stt", [P, 2, T])
        prod = sb("prod", [P, 2, T])
        zs = sb("zs", [P, T])
        pm = sb("pm", [P, QB, DG])
        mx = sb("mx", [P, QB])
        sm = sb("sm", [P, QB])
        ri = sb("ri", [P, QB])
        prr = sb("prr", [P, QB, KK, DG])
        prep = sb("prep", [P, T])

        ld, wt_mm, wt_cp = sem("c_ld"), sem("c_wt_mm"), sem("c_wt_cp")
        rsq_done, rms_mm, rln_done, rrs_done, rms_done = (sem("c_rsq_done"), sem("c_rms_mm"), sem("c_rln_done"),
                                                          sem("c_rrs_done"), sem("c_rms_done"))
        pr_mm, pr_cp, f_step = sem("c_pr_mm"), sem("c_pr_cp"), sem("c_f_step")

        def rms_act(act, n, src):
            act.preload_act_table_set("natural_log_exp_and_others")
            for k in range(NC):
                act.activation(sqr[:, k, :], src(k), ACT.Square).then_inc(rsq_done, 1)
            for k in range(NC):
                act.wait_ge(rms_mm, NC * n + k + 1)
                act.activation(rstd[:, k, :], bank[4 + k], ACT.Ln, bias=ln_eps[:, 0:1]).then_inc(rln_done, 1)
            for k in range(NC):
                act.wait_ge(rln_done, NC * n + k + 1)
                act.activation(rstd[:, k, :], rstd[:, k, :], ACT.Exp, scale=-0.5).then_inc(rrs_done, 1)

        def rms_pe(pe, n):
            for k in range(NC):
                pe.wait_ge(rsq_done, NC * n + k + 1)
                pe.matmul(bank[4 + k], jmean[:, :], sqr[:, k, :], start=True, stop=True).then_inc(rms_mm, 1)

        def rms_dve(dve, n, t):
            for k in range(NC):
                dve.wait_ge(rrs_done, NC * n + k + 1)
                dve.scalar_tensor_tensor(out=t(k), in0=t(k), scalar=gains[:, n:n + 1], in1=rstd[:, k, :],
                                         op0=ALU.mult, op1=ALU.mult).then_inc(rms_done, 1)

        with nc.Block() as block:
            @block.sync
            def _(sp):
                for i, nm in enumerate(names):
                    sp.dma_start(wtok[:, i, :], w["L0_attn_b_" + nm]).then_inc(ld, 16)
                for i, nm in enumerate(("norm_weight", "gnorm_weight")):
                    sp.dma_start(gains[:, i:i + 1], w["L0_attn_b_" + nm].rearrange("(p a) -> p a", a=1)).then_inc(ld, 16)
                for dst, nm in ((hmask[:, :], "c_hmask"), (pick[:, :, :], "c_pick"), (put[:, :, :], "c_put"),
                                (spread[:, :], "c_spread")):
                    sp.dma_start(dst, c[nm]).then_inc(ld, 16)

            @block.tensor
            def _(pe):
                ln_pe(pe, ln_call, lambda k: xT[:, cs(k)])
                rms_pe(pe, 0)
                pe.wait_ge(ld, 16 * 11)
                for i in range(5):
                    o = bank[i // 4]
                    m = pe.transpose(o[:, (i % 4) * P:(i % 4 + 1) * P], wtok[:, i, :], ident[:, :])
                m.then_inc(wt_mm, 1)
                pe.wait_ge(wt_cp, 2)
                pe.wait_ge(rms_done, NC)
                for k in range(NC):
                    for i in range(4):
                        if k:
                            pe.wait_ge(pr_cp, 4 * (k - 1) + i + 1)
                        pe.matmul(bank[i][:, :], wT[:, i, :], y[:, cs(k)], start=True, stop=True).then_inc(pr_mm, 1)

            @block.scalar
            def _(act):
                ln_act(act, ln_call)
                act.wait_ge(norm_done, NC * (ln_call + 1))
                rms_act(act, 0, lambda k: y[:, cs(k)])
                act.wait_ge(wt_mm, 1)
                act.activation(wT[:, 0:4, :], bank[0][:, :].rearrange("p (i d) -> p i d", i=4), ACT.Copy).then_inc(wt_cp, 1)
                act.activation(wT[:, 4, :], bank[1][:, 0:P], ACT.Copy).then_inc(wt_cp, 1)
                for k in range(NC):
                    for i in range(4):
                        act.wait_ge(pr_mm, 4 * k + i + 1)
                        if i < 3:
                            act.activation(qkv[:, i, cs(k)], bank[i][:, :], ACT.Silu).then_inc(pr_cp, 1)
                        else:
                            act.activation(f[:, cs(k)], bank[i][:, :], ACT.Copy).then_inc(pr_cp, 1)
                act.wait_ge(pr_cp, 4 * NC)
                act.activation(e[:, :], f[:, :], ACT.Abs).then_inc(f_step, 1)
                act.wait_ge(f_step, 1)
                act.activation(e[:, :], e[:, :], ACT.Exp, scale=-1.0).then_inc(f_step, 1)
                act.wait_ge(f_step, 2)
                act.activation(e[:, :], e[:, :], ACT.Ln, bias=1.0).then_inc(f_step, 1)
                act.wait_ge(f_step, 4)
                act.activation(e[:, :], f[:, :], ACT.Tanh, scale=-1.0 / 32).then_inc(f_step, 1)

            @block.vector
            def _(dve):
                ln_dve(dve, ln_call, lambda k: xT[:, cs(k)], lambda k: y[:, cs(k)])
                dve.wait_ge(norm_done, NC * (ln_call + 1))
                dve.wait_ge(ld, 16 * 11)
                rms_dve(dve, 0, lambda k: y[:, cs(k)])
                dve.memset(oT[:, :], 0.0)
                dve.wait_ge(f_step, 3)
                dve.scalar_tensor_tensor(out=f[:, :], in0=f[:, :], scalar=0.0, in1=e[:, :], op0=ALU.min,
                                         op1=ALU.subtract).then_inc(f_step, 1)
                dve.wait_ge(f_step, 5)
                dve.tensor_scalar(f[:, :], e[:, :], 1.0, None, ALU.add).then_inc(f_step, 1)
                dve.wait_ge(f_step, 6)
                dve.reciprocal(f[:, :], f[:, :]).then_inc(f_step, 1)
                dve.wait_ge(f_step, 7)
                dve.scalar_tensor_tensor(out=s[:, :], in0=e[:, :], scalar=2.0, in1=f[:, :], op0=ALU.mult,
                                         op1=ALU.mult).then_inc(f_step, 1)

        own_done, rep_mm, rep_cp = sem("c_own_done"), sem("c_rep_mm"), sem("c_rep_cp")
        in_mm, in_done, scan_done, qb_mm, prod_done, red_mm = (sem("c_in_mm"), sem("c_in_done"), sem("c_scan_done"),
                                                               sem("c_qb_mm"), sem("c_prod_done"), sem("c_red_mm"))
        z_cp, zt_mm, p_step, pt_mm, prep_done, acc_done = (sem("c_z_cp"), sem("c_zt_mm"), sem("c_p_step"), sem("c_pt_mm"),
                                                           sem("c_prep_done"), sem("c_acc_done"))
        R = 2 * KG
        with nc.Block() as block:
            @block.gpsimd
            def _(pool):
                for t in (in_done, prod_done, acc_done, in_mm, scan_done):
                    pool.sem_inc(t, ONE)

            @block.tensor
            def _(pe):
                with pe.Fori(0, B) as b:
                    with pe.Fori(0, HG) as h:
                        g = b * HG + h
                        pe.wait_ge(own_done, 4 * g + 4)
                        pe.wait_ge(acc_done, ONE + 2 * g)
                        for a in range(2):
                            pe.matmul(bank[2 + a][:, :], spread[:, :], own[:, 3, cs(a)], start=True, stop=True).then_inc(rep_mm, 1)

                        def enter(r, pe=pe, g=g):
                            pe.wait_ge(in_done, ONE + R * g + r)
                            for a in range(2):
                                m = pe.matmul(bank[4 + a], pick[:, r % KG, :], own[:, 1 if r < KG else 2, cs(a)],
                                              start=True, stop=True)
                            m.then_inc(in_mm, 1)

                        def query(r, pe=pe, g=g):
                            pe.wait_ge(prod_done, ONE + R * g + r)
                            for a in range(2):
                                m = pe.matmul(bank[6 + a], pick[:, r, :], own[:, 0, cs(a)], start=True, stop=True)
                            m.then_inc(qb_mm, 1)

                        def gather(r, pe=pe, g=g):
                            pe.wait_ge(prod_done, ONE + R * g + r + 1)
                            for a in range(2):
                                m = pe.matmul(bank[a][:, :], spread[:, :] if r < KG else put[:, r % KG, :], prod[:, r % 2, cs(a)],
                                              start=(r % KG == 0), stop=(r % KG == KG - 1), skip_group_check=True)
                            m.then_inc(red_mm, 1)
                        enter(0)
                        query(0)
                        for r in range(KG):
                            enter(r + 1)
                            if r + 1 < KG:
                                query(r + 1)
                            gather(r)
                        pe.wait_ge(z_cp, 2 * g + 2)
                        pe.wait_ge(rep_cp, 4 * g + 4)
                        for i in range(QB):
                            m = pe.transpose(bank[2 + i // 4][:, (i % 4) * P:(i % 4 + 1) * P], zs[:, i * P:(i + 1) * P], ident[:, :])
                        m.then_inc(zt_mm, 1)
                        pe.wait_ge(p_step, 6 * g + 6)
                        for i in range(QB):
                            m = pe.transpose(bank[2 + i // 4][:, (i % 4) * P:(i % 4 + 1) * P],
                                             prr[:, i, :, :].rearrange("p k m -> p (k m)"), ident[:, :])
                        m.then_inc(pt_mm, 1)
                        for r in range(KG, R):
                            if r + 1 < R:
                                enter(r + 1)
                            gather(r)

            @block.scalar
            def _(act):
                act.sem_inc(red_mm, 2)
                with act.Fori(0, B) as b:
                    with act.Fori(0, HG) as h:
                        g = b * HG + h
                        act.wait_ge(in_mm, ONE + R * g)
                        for i in range(4):
                            src = qkv[:, i, bass.ds(b * T, T)] if i < 3 else s[:, bass.ds(b * T, T)]
                            act.activation(own[:, i, :], src, ACT.Copy, scale=hmask[:, bass.ds(h, 1)]).then_inc(own_done, 1)
                        act.wait_ge(scan_done, ONE + R * g)
                        for a in range(2):
                            act.wait_ge(rep_mm, 2 * g + a + 1)
                            act.activation(srep[:, cs(a)], bank[2 + a][:, :], ACT.Copy).then_inc(rep_cp, 1)
                            act.activation(lrep[:, cs(a)], bank[2 + a][:, :], ACT.Identity, bias=1.0, scale=-1.0).then_inc(rep_cp, 1)
                        act.wait_ge(red_mm, R * g + KG + 2)
                        for a in range(2):
                            act.activation(zs[:, cs(a)], bank[a][:, :], ACT.Copy).then_inc(z_cp, 1)
                        act.wait_ge(p_step, 6 * g + 2)
                        act.activation(pm[:, :, :], pm[:, :, :], ACT.Exp).then_inc(p_step, 1)
                        act.wait_ge(pt_mm, g + 1)
                        for a in range(2):
                            act.activation(prep[:, cs(a)], bank[2 + a][:, :], ACT.Copy).then_inc(prep_done, 1)

            @block.vector
            def _(dve):
                with dve.Fori(0, B) as b:
                    with dve.Fori(0, HG) as h:
                        g = b * HG + h
                        dve.wait_ge(rep_cp, 4 * g + 4)

                        def tile(r, dve=dve, g=g):
                            n = R * g + r
                            dve.wait_ge(in_mm, ONE + n + 1)
                            dve.tensor_tensor(inp[:, r % 2, :], wide[0][:, :], srep[:, :], ALU.mult).then_inc(in_done, 1)
                            dve.wait_ge(in_done, ONE + n + 1)
                            dve.tensor_tensor_scan(stt[:, r % 2, :], lrep[:, :], inp[:, r % 2, :], 0.0, ALU.mult, ALU.add)\
                                .then_inc(scan_done, 1)
                            if r < KG:
                                dve.wait_ge(qb_mm, KG * g + r + 1)
                            elif r == KG:
                                dve.wait_ge(prep_done, 2 * g + 2)
                            dve.wait_ge(red_mm, n + 1)
                            dve.wait_ge(scan_done, ONE + n + 1)
                            dve.tensor_tensor(prod[:, r % 2, :], wide[1][:, :] if r < KG else prep[:, :], stt[:, r % 2, :],
                                              ALU.mult).then_inc(prod_done, 1)
                        for r in range(KG):
                            tile(r)
                        dve.wait_ge(zt_mm, g + 1)
                        for a in range(2):
                            z = bank[2 + a][:, :].rearrange("p (i c) -> p i c", i=4)[:, :, 0:DG]
                            m = dve.tensor_reduce(mx[:, 4 * a:4 * a + 4], z, AX.X, ALU.max)
                        m.then_inc(p_step, 1)
                        dve.wait_ge(p_step, 6 * g + 1)
                        for a in range(2):
                            z = bank[2 + a][:, :].rearrange("p (i c) -> p i c", i=4)[:, :, 0:DG]
                            m = dve.tensor_tensor(pm[:, 4 * a:4 * a + 4, :], z, mx[:, 4 * a:4 * a + 4].rearrange("p (i a) -> p i a", a=1)
                                                  .broadcast_to([P, 4, DG]), ALU.subtract)
                        m.then_inc(p_step, 1)
                        dve.wait_ge(p_step, 6 * g + 3)
                        dve.tensor_reduce(sm[:, :], pm[:, :, :], AX.X, ALU.add).then_inc(p_step, 1)
                        dve.wait_ge(p_step, 6 * g + 4)
                        dve.reciprocal(ri[:, :], sm[:, :]).then_inc(p_step, 1)
                        dve.wait_ge(p_step, 6 * g + 5)
                        for k in range(KK):
                            m = dve.tensor_tensor(prr[:, :, k, :], pm[:, :, :], ri[:, :].rearrange("p (i a) -> p i a", a=1)
                                                  .broadcast_to([P, QB, DG]), ALU.mult)
                        m.then_inc(p_step, 1)
                        for r in range(KG, R):
                            tile(r)
                        dve.wait_ge(red_mm, R * g + R + 2)
                        for a in range(2):
                            o = oT[:, bass.ds(b * T + a * CH, CH)]
                            dve.scalar_tensor_tensor(out=o, in0=bank[a][:, :], scalar=hmask[:, bass.ds(h, 1)], in1=o,
                                                     op0=ALU.mult, op1=ALU.add).then_inc(acc_done, 1)

        sw_done, o_mm, o_add = sem("c_sw_done"), sem("c_o_mm"), sem("c_o_add")
        with nc.Block() as block:
            @block.scalar
            def _(act):
                for k in range(NC):
                    act.activation(oT[:, cs(k)], oT[:, cs(k)], ACT.Silu).then_inc(sw_done, 1)
                act.wait_ge(sw_done, NC)
                rms_act(act, 1, lambda k: oT[:, cs(k)])

            @block.tensor
            def _(pe):
                rms_pe(pe, 1)
                for k in range(NC):
                    pe.wait_ge(rms_done, NC + k + 1)
                    pe.matmul(bank[k][:, :], wT[:, 4, :], oT[:, cs(k)], start=True, stop=True).then_inc(o_mm, 1)

            @block.vector
            def _(dve):
                dve.wait_ge(sw_done, NC)
                rms_dve(dve, 1, lambda k: oT[:, cs(k)])
                for k in range(NC):
                    dve.wait_ge(o_mm, k + 1)
                    dve.tensor_tensor(xT[:, cs(k)], bank[k][:, :], xT[:, cs(k)], ALU.add).then_inc(o_add, 1)


def constants():
    import numpy as np
    bf = np.dtype("bfloat16")
    t = {"ident": np.eye(P, dtype=np.float32), "identb": np.eye(P).astype(bf),
         "jmean": np.full((P, P), 1 / D, np.float32)}
    head = np.arange(D) // (D // HA)
    own = (head[:, None] == np.arange(HA)[None, :])
    t["a_hmask"] = (own * D ** -0.5).astype(np.float32)
    t["a_cmask"] = np.broadcast_to(own.T[None], (P, HA, D)).astype(np.float32)
    i = np.arange(P)
    t["a_dmask"] = np.where(i[:, None] >= i[None, :], 0.0, NEG).astype(bf)
    half = np.arange(0, DH, 2, dtype=np.float32)
    inv = (1.0 / 10000.0 ** (half / DH)).astype(np.float32)
    pos = np.arange(T, dtype=np.float32)
    ang = (pos[:, None] * inv[None, :]).astype(np.float32)
    ang = np.concatenate([ang, ang], -1).astype(np.float64)
    base = ((half + 0.4 * DH) / (1.4 * DH)).astype(np.float32)
    power = (pos - T // 2) / (WIN // 2)
    scale = base[None, :].astype(np.float64) ** power[:, None]
    scale = np.concatenate([scale, scale], -1)
    sign = np.where(np.arange(DH) < DH // 2, 1.0, -1.0)
    tabs = [np.cos(ang) * scale, np.sin(ang) * scale * sign, np.cos(ang) / scale, np.sin(ang) / scale * sign]
    t["rot"] = np.stack([np.concatenate([x.T, x.T], 0) for x in tabs], 1).astype(np.float32).copy()
    blk = np.arange(P) // DH
    t["same_head"] = (blk[:, None] == blk[None, :]).astype(np.float32)
    q, k = np.arange(P)[:, None] % BLK, np.arange(KEYS)[None, :] - WIN
    seen = (q >= k) & (q - k <= WIN)
    m = np.where(seen, 0.0, NEG)
    m0 = np.where(seen & (k >= 0), 0.0, NEG)
    t["band"] = np.stack([np.concatenate([m0, m, m, m], 1), np.concatenate([m] * 4, 1)], 1).astype(bf).copy()
    f = np.arange(P)
    t["c_hmask"] = (f[:, None] // DG == np.arange(HG)[None, :]).astype(np.float32)
    t["c_pick"] = np.stack([(f[:, None] % DG == KK * g + f[None, :] // DG) for g in range(KG)], 1).astype(np.float32).copy()
    t["c_put"] = np.stack([(f[None, :] % DG == KK * g + f[:, None] // DG) for g in range(KG)], 1).astype(np.float32).copy()
    t["c_spread"] = (f[:, None] % DG == f[None, :] % DG).astype(np.float32)
    return t


def kernel(**inputs):
    import numpy as _np
    import concourse.bacc as _bacc
    from concourse import mybir as _mybir
    from concourse.bass_utils import run_bass_kernel_spmd as _run

    nc = _bacc.Bacc("TRN2", target_bir_lowering=False, num_devices=1)
    arrays, w, c = {}, {}, {}
    for group, named in ((w, inputs), (c, constants())):
        for name, a in named.items():
            a = _np.ascontiguousarray(a)
            arrays[f"in_{name}"] = a
            group[name] = nc.dram_tensor(f"in_{name}", a.shape, _mybir.dt.from_np(a.dtype), kind="ExternalInput").ap()
    out = nc.dram_tensor("out_0", (B, T, D), _mybir.dt.float32, kind="ExternalOutput").ap()
    hybrid_kernel(nc, w, c, out)
    r = _run(nc, [arrays], core_ids=[0])
    return r.results[0]["out_0"]
```

```python
from contextlib import ExitStack

import concourse.bass as bass
from concourse import mybir

F32 = mybir.dt.float32
BF16 = mybir.dt.bfloat16
F32R = mybir.dt.float32r
ALU = mybir.AluOpType
ACT = mybir.ActivationFunctionType
AX = mybir.AxisListType

P = 128
B, T, D = 2, 1024, 128
N = B * T
CH = 512
NC = N // CH
LN_EPS = 1e-5

HA = 16
QB = T // P
DEPTH, HEADS, DH, WIN = 6, 16, 64, 32
INNER = HEADS * DH
PAIRS = HEADS // 2
BLK = 64
NB = CH // BLK
KEYS = BLK + WIN
QK_SCALE = 8.0
FI = int(D * 4 * 2 / 3)
FT = -(-FI // P)
FR = FI - (FT - 1) * P
HG, DG = 4, 32
KK = P // DG
KG = DG // KK
NEG = -1e30
SS_SCALE = 2.0 ** 16
SS_EPS = 1e-24 * SS_SCALE
SS_BACK = 8 * 0.6931471805599453
ONE = 1


def pipelined(eng, per, count, lag, slot, peel_last=False):
    def run(it, first=False, end=False):
        for j in range(lag if end else per):
            def unit(k, j=j):
                back, jj = divmod(j - k, per)
                if (first and back < 0) or (end and back >= 0):
                    return None
                return it + back, jj
            slot(j, unit)
    assert lag <= per
    run(0, first=True)
    with eng.Fori(1, count - 1 if peel_last else count) as it:
        run(it)
    if peel_last:
        run(count - 1)
    run(count, end=True)


def hybrid_kernel(nc, w, c, out):
    ctx = ExitStack()
    scope = [ctx]

    def sb(name, shape, dt=F32):
        return scope[0].enter_context(nc.sbuf_tensor(name, shape, dt))

    def sem(name):
        return ctx.enter_context(nc.semaphore(name))

    with ctx:
        bank = [ctx.enter_context(nc.psum_tensor(f"bank{i}", [P, CH], F32)) for i in range(4)]
        wide = [ctx.enter_context(nc.psum_tensor(f"wide{i}", [P, 2 * CH], F32)) for i in range(2)]
        bank += [wide[0][:, 0:CH], wide[0][:, CH:2 * CH], wide[1][:, 0:CH], wide[1][:, CH:2 * CH]]
        xT = sb("xT", [P, N])
        y = sb("y", [P, N])
        ident = sb("ident", [P, P])
        identb = sb("identb", [P, P], BF16)
        jmean = sb("jmean", [P, P])
        cen = sb("cen", [P, NC, CH])
        sqr = sb("sqr", [P, NC, CH])
        rstd = sb("rstd", [P, NC, CH])

        const_ld = sem("const_ld")
        x_ld, tin_mm, tin_cp = sem("x_ld"), sem("tin_mm"), sem("tin_cp")
        mean_mm, cen_done, sqr_done, var_mm = sem("mean_mm"), sem("cen_done"), sem("sqr_done"), sem("var_mm")
        lnv_done, rstd_done, norm_done = sem("lnv_done"), sem("rstd_done"), sem("norm_done")

        def cs(k):
            return slice(k * CH, (k + 1) * CH)

        def ln_pe(pe, n, src, ready=None):
            for k in range(NC + 1):
                if k < NC:
                    if ready:
                        ready(pe, k)
                    pe.matmul(bank[k][:, :], jmean[:, :], src(k), start=True, stop=True).then_inc(mean_mm, 1)
                if k:
                    pe.wait_ge(sqr_done, NC * n + k)
                    pe.matmul(bank[3 + k], jmean[:, :], sqr[:, k - 1, :], start=True, stop=True).then_inc(var_mm, 1)

        def ln_act(act, n, after=None):
            act.preload_act_table_set("natural_log_exp_and_others")
            for k in range(NC + 2):
                if k < NC:
                    act.wait_ge(cen_done, NC * n + k + 1)
                    act.activation(sqr[:, k, :], cen[:, k, :], ACT.Square).then_inc(sqr_done, 1)
                if 0 < k <= NC:
                    act.wait_ge(var_mm, NC * n + k)
                    act.activation(rstd[:, k - 1, :], bank[3 + k], ACT.Ln, bias=ln_eps[:, 0:1]).then_inc(lnv_done, 1)
                    act.wait_ge(lnv_done, NC * n + k)
                    act.activation(rstd[:, k - 1, :], rstd[:, k - 1, :], ACT.Exp, scale=-0.5).then_inc(rstd_done, 1)
                if k > 1 and after:
                    after(act, k - 2)

        def ln_dve(dve, n, src, dst, gain=None):
            for k in range(NC + 2):
                if k < NC:
                    dve.wait_ge(mean_mm, NC * n + k + 1)
                    dve.tensor_tensor(cen[:, k, :], src(k), bank[k][:, :], ALU.subtract).then_inc(cen_done, 1)
                if k > 1:
                    i = k - 2
                    dve.wait_ge(rstd_done, NC * n + i + 1)
                    if gain is None:
                        dve.tensor_tensor(dst(i), cen[:, i, :], rstd[:, i, :], ALU.mult).then_inc(norm_done, 1)
                    else:
                        dve.scalar_tensor_tensor(out=dst(i), in0=cen[:, i, :], scalar=gain, in1=rstd[:, i, :],
                                                 op0=ALU.mult, op1=ALU.mult).then_inc(norm_done, 1)

        ln_eps = sb("ln_eps", [P, 1])
        ss_eps = sb("ss_eps", [P, 1])
        ss_back = sb("ss_back", [P, 1])
        eps_set = sem("eps_set")

        with ExitStack() as inner:
            scope[0] = inner
            xtok = sb("xtok", [P, N // P, D])
            with nc.Block() as block:
                @block.sync
                def _(sp):
                    for n, (dst, src) in enumerate(((ident[:, :], c["ident"]), (identb[:, :], c["identb"]),
                                                    (jmean[:, :], c["jmean"]))):
                        sp.dma_start(dst, src).then_inc(const_ld, 16)
                    sp.dma_start(xtok[:, :, :], w["L0_attn_a_x"].rearrange("b (n p) d -> p (b n) d", p=P))\
                        .then_inc(x_ld, 16)

                @block.tensor
                def _(pe):
                    pe.wait_ge(const_ld, 48)
                    pe.wait_ge(x_ld, 16)
                    for k in range(NC):
                        for i in range(4):
                            m = pe.transpose(bank[k][:, i * P:(i + 1) * P], xtok[:, 4 * k + i, :], ident[:, :])
                        m.then_inc(tin_mm, 1)

                @block.scalar
                def _(act):
                    for k in range(NC):
                        act.wait_ge(tin_mm, k + 1)
                        act.activation(xT[:, cs(k)], bank[k][:, :], ACT.Copy).then_inc(tin_cp, 1)

                @block.vector
                def _(dve):
                    dve.memset(ln_eps[:, :], LN_EPS).then_inc(eps_set, 1)
                    dve.memset(ss_eps[:, :], SS_EPS).then_inc(eps_set, 1)
                    dve.memset(ss_back[:, :], SS_BACK).then_inc(eps_set, 1)
            scope[0] = ctx

        stage_a(nc, w, c, sem, bank, wide, xT, y, ident, identb, ln_pe, ln_act, ln_dve, cs, 0)
        S = stack_semaphores(sem)
        common = (S, nc, w, c, bank, wide, xT, y, ident, identb, ln_eps, ss_eps, ss_back,
                  ln_pe, ln_act, ln_dve, norm_done, cs, cen)
        stack(0, 1, *common)
        stage_c(nc, w, c, sem, bank, wide, xT, y, ident, jmean, ln_eps, sqr, rstd, ln_pe, ln_act, ln_dve, norm_done, cs, 8)
        stack(1, 9, *common)

        out_mm, out_cp, out_st = sem("out_mm"), sem("out_cp"), sem("out_st")
        with ExitStack() as inner:
            scope[0] = inner
            otok = sb("otok", [P, N // P, D])
            with nc.Block() as block:
                @block.tensor
                def _(pe):
                    for k in range(NC):
                        for i in range(4):
                            m = pe.transpose(bank[k][:, i * P:(i + 1) * P],
                                             xT[:, (4 * k + i) * P:(4 * k + i + 1) * P], ident[:, :])
                        m.then_inc(out_mm, 1)

                @block.scalar
                def _(act):
                    for k in range(NC):
                        act.wait_ge(out_mm, k + 1)
                        act.activation(otok[:, 4 * k:4 * k + 4, :],
                                       bank[k][:, :].rearrange("p (i d) -> p i d", i=4), ACT.Copy).then_inc(out_cp, 1)

                @block.sync
                def _(sp):
                    ov = out.rearrange("b (n p) d -> p (b n) d", p=P)
                    for k in range(NC):
                        sp.wait_ge(out_cp, k + 1)
                        sp.dma_start(ov[:, 4 * k:4 * k + 4, :], otok[:, 4 * k:4 * k + 4, :]).then_inc(out_st, 16)
                    sp.wait_ge(out_st, 16 * NC)
            scope[0] = ctx


def stage_a(nc, w, c, sem, bank, wide, xT, y, ident, identb, ln_pe, ln_act, ln_dve, cs, ln_call):
    with ExitStack() as st:
        def sb(name, shape, dt=F32):
            return st.enter_context(nc.sbuf_tensor(name, shape, dt))

        wtok = sb("a_wtok", [P, 4, D])
        wT = sb("a_wT", [P, 4, D])
        bias = sb("a_bias", [P, 4])
        hmask = sb("a_hmask", [P, HA])
        cmask = sb("a_cmask", [P, HA, D])
        dmask = sb("a_dmask", [P, P], BF16)
        zero = sb("a_zero", [P, CH], BF16)
        qT = sb("a_qT", [P, N])
        kT = sb("a_kT", [P, N])
        v = sb("a_v", [P, N // P, D])
        qm = sb("a_qm", [P, T])
        vm = sb("a_vm", [P, QB, D])
        prob = sb("a_prob", [P, 4, T])
        pT = sb("a_pT", [P, 2, QB, P])
        nmax = sb("a_nmax", [P, 4])
        rsum = sb("a_rsum", [P, 4])
        rinv = sb("a_rinv", [P, 4])
        oT = sb("a_oT", [P, T])
        a_ld = sem("a_ld")
        wt_mm, wt_cp, zero_set = sem("a_wt_mm"), sem("a_wt_cp"), sem("a_zero_set")
        pr_mm, pr_cp = sem("a_pr_mm"), sem("a_pr_cp")

        norm_done = sem("a_normed")

        def hT(k):
            return y[:, cs(k)]

        with nc.Block() as block:
            @block.sync
            def _(sp):
                for i, nm in enumerate("qkvo"):
                    sp.dma_start(wtok[:, i, :], w[f"L0_attn_a_W{nm}_w"]).then_inc(a_ld, 16)
                    sp.dma_start(bias[:, i:i + 1], w[f"L0_attn_a_W{nm}_b"].rearrange("(p a) -> p a", a=1))\
                        .then_inc(a_ld, 16)
                for dst, src in ((hmask[:, :], c["a_hmask"]), (cmask[:, :, :], c["a_cmask"]), (dmask[:, :], c["a_dmask"])):
                    sp.dma_start(dst, src).then_inc(a_ld, 16)

            @block.tensor
            def _(pe):
                ln_pe(pe, ln_call, lambda k: xT[:, cs(k)])
                pe.wait_ge(a_ld, 16 * 11)
                pe.wait_ge(norm_done, 1)
                for i in range(4):
                    m = pe.transpose(bank[0][:, i * P:(i + 1) * P], wtok[:, i, :], ident[:, :])
                m.then_inc(wt_mm, 1)
                pe.wait_ge(wt_cp, 1)
                for k in range(NC):
                    for i in range(3):
                        n = 3 * k + i
                        o = bank[1 + n % 6] if n % 6 > 2 else bank[1 + n % 6][:, :]
                        if n >= 6:
                            pe.wait_ge(pr_cp, n - 5)
                        if i < 2:
                            m = pe.matmul(o, wT[:, i, :], hT(k), start=True, stop=True)
                        else:
                            for t in range(4):
                                m = pe.matmul(o[:, t * P:(t + 1) * P], y[:, (4 * k + t) * P:(4 * k + t + 1) * P],
                                              wT[:, 2, :], start=(t == 0), stop=(t == 3), skip_group_check=True)
                        m.then_inc(pr_mm, 1)

            @block.scalar
            def _(act):
                ln_act(act, ln_call)
                act.wait_ge(wt_mm, 1)
                act.activation(wT[:, :, :], bank[0][:, :].rearrange("p (i d) -> p i d", i=4), ACT.Copy).then_inc(wt_cp, 1)
                for n in range(3 * NC):
                    k, i = divmod(n, 3)
                    src = bank[1 + n % 6] if n % 6 > 2 else bank[1 + n % 6][:, :]
                    act.wait_ge(pr_mm, n + 1)
                    if i < 2:
                        act.activation((qT, kT)[i][:, cs(k)], src, ACT.Identity, bias=bias[:, i:i + 1]).then_inc(pr_cp, 1)
                    else:
                        act.activation(v[:, 4 * k:4 * k + 4, :], src.rearrange("p (t d) -> p t d", t=4), ACT.Copy)\
                            .then_inc(pr_cp, 1)

            @block.vector
            def _(dve):
                dve.memset(zero[:, :], 0.0).then_inc(zero_set, 1)
                ln_dve(dve, ln_call, lambda k: xT[:, cs(k)], hT)
                dve.drain().then_inc(norm_done, 1)

        s_mm, smax_done, exp_done = sem("a_s_mm"), sem("a_smax_done"), sem("a_exp_done")
        rinv_done, pn_done = sem("a_rinv_done"), sem("a_pn_done")
        t_mm = [sem("a_t_mm0"), sem("a_t_mm1")]
        pt_cp = [sem("a_pt_cp0"), sem("a_pt_cp1")]
        pv_mm = sem("a_pv_mm")
        qm_done, vm_done = sem("a_qm_done"), sem("a_vm_done")
        o_cp, wo_mm, res_done = sem("a_o_cp"), sem("a_wo_mm"), sem("a_res_done")
        units = HA * QB
        LAG = 2
        SC, PR = 2, 4
        scores = [wide[0], wide[1]]
        turned = [bank[0], bank[1]]
        oacc = [bank[2], bank[3]]

        def at(b, u):
            return units * b + QB * u[0] + u[1], HA * b + u[0], u[1]

        def grp(a, n, g, i):
            return n + 1 if a == 0 else 4 * g + i - 3

        with nc.Block() as block:
            @block.tensor
            def _(pe):
                for b in range(B):
                    if b:
                        pe.wait_ge(o_cp, 2 * b)
                        pe.wait_ge(res_done, 2 * b)
                    for a in range(2):
                        pe.matmul(oacc[a][:, :], zero[:, 0:P], zero[:, :], start=True, stop=False, skip_group_check=True)

                    def slot(j, unit, b=b):
                        u = unit(0)
                        if u:
                            n, g, i = at(b, u)
                            s = scores[i % SC]
                            if i == 0:
                                pe.wait_ge(qm_done, g + 1)
                            pe.wait_ge(exp_done, n + 1)
                            for a in range((i + 4) // 4):
                                e = min(CH * (a + 1), P * (i + 1))
                                pe.matmul(s[:, CH * a:e], qm[:, i * P:(i + 1) * P], kT[:, b * T + CH * a:b * T + e],
                                          start=True, stop=False, skip_group_check=True)
                            pe.matmul(s[:, i * P:(i + 1) * P], identb[:, :], dmask[:, :],
                                      start=False, stop=True, skip_group_check=True).then_inc(s_mm, 1)
                        u = unit(LAG)
                        if u:
                            n, g, i = at(b, u)
                            if i == 0:
                                pe.wait_ge(vm_done, g + 1)
                            pe.wait_ge(pn_done, n + 1)
                            for a in range((i + 4) // 4):
                                pe.wait_ge(pt_cp[a], grp(a, n, g, i) - 1)
                                for kb in range(4 * a, min(4 * a + 4, i + 1)):
                                    m = pe.transpose(turned[a][:, (kb % 4) * P:(kb % 4 + 1) * P],
                                                     prob[:, i % PR, kb * P:(kb + 1) * P], ident[:, :])
                                m.then_inc(t_mm[a], 1)
                            for kb in range(i + 1):
                                if kb % 4 == 0:
                                    pe.wait_ge(pt_cp[kb // 4], grp(kb // 4, n, g, i))
                                m = pe.matmul(oacc[i // 4][:, (i % 4) * P:(i % 4 + 1) * P], vm[:, kb, :],
                                              pT[:, i % 2, kb, :], start=False, stop=False, skip_group_check=True)
                            m.then_inc(pv_mm, 1)
                    pipelined(pe, QB, HA, LAG, slot)
                    for a in range(2):
                        pe.wait_ge(o_cp, 2 * b + a + 1)
                        pe.matmul(scores[0][:, a * CH:(a + 1) * CH], wT[:, 3, :], oT[:, a * CH:(a + 1) * CH],
                                  start=True, stop=True).then_inc(wo_mm, 1)

            @block.scalar
            def _(act):
                act.sem_inc(exp_done, SC)
                for b in range(B):
                    def slot(j, unit, b=b):
                        u = unit(0)
                        if u:
                            n, g, i = at(b, u)
                            act.wait_ge(smax_done, n + 1)
                            act.wait_ge(pv_mm, n + 1)
                            e = P * (i + 1)
                            act.activation(prob[:, i % PR, 0:e], scores[i % SC][:, 0:e], ACT.Exp, bias=nmax[:, i % 4:i % 4 + 1],
                                           accum_out=rsum[:, i % 4:i % 4 + 1]).then_inc(exp_done, 1)
                        u = unit(LAG)
                        if u:
                            n, g, i = at(b, u)
                            act.wait_ge(pv_mm, n + 1 + PR - 2)
                            for a in range((i + 4) // 4):
                                k = min(4, i + 1 - 4 * a)
                                act.wait_ge(t_mm[a], grp(a, n, g, i))
                                act.activation(pT[:, i % 2, 4 * a:4 * a + k, :],
                                               turned[a][:, 0:k * P].rearrange("p (k q) -> p k q", k=k), ACT.Copy)\
                                    .then_inc(pt_cp[a], 1)
                    pipelined(act, QB, HA, LAG, slot)
                    act.wait_ge(pv_mm, units * (b + 1) + PR)
                    if b:
                        act.wait_ge(wo_mm, 2 * b)
                    for a in range(2):
                        act.activation(oT[:, a * CH:(a + 1) * CH], oacc[a][:, :], ACT.Identity, bias=bias[:, 2:3])\
                            .then_inc(o_cp, 1)

            @block.gpsimd
            def _(pool):
                pool.sem_inc(pv_mm, PR)
                for b in range(B):
                    with pool.Fori(0, HA) as h:
                        pool.wait_ge(pv_mm, units * b + QB * h + PR)
                        pool.tensor_tensor(vm[:, :, :], v[:, QB * b:QB * b + QB, :],
                                           cmask[:, bass.ds(h, 1), :].broadcast_to([P, QB, D]), ALU.mult).then_inc(vm_done, 1)

            @block.vector
            def _(dve):
                for b in range(B):
                    def slot(j, unit, b=b):
                        u = unit(0)
                        if u:
                            n, g, i = at(b, u)
                            if i == 0:
                                dve.wait_ge(s_mm, n)
                                dve.tensor_scalar(qm[:, :], qT[:, b * T:(b + 1) * T], hmask[:, bass.ds(u[0], 1)], None, ALU.mult)\
                                    .then_inc(qm_done, 1)
                            dve.wait_ge(s_mm, n + 1)
                            dve.wait_ge(exp_done, n + 1)
                            dve.tensor_reduce(nmax[:, i % 4:i % 4 + 1], scores[i % SC][:, 0:P * (i + 1)], AX.X, ALU.max,
                                              negate=True).then_inc(smax_done, 1)
                        u = unit(1)
                        if u:
                            n, g, i = at(b, u)
                            dve.wait_ge(exp_done, n + 1 + SC)
                            dve.reciprocal(rinv[:, i % 4:i % 4 + 1], rsum[:, i % 4:i % 4 + 1]).then_inc(rinv_done, 1)
                            dve.wait_ge(rinv_done, n + 1)
                            dve.tensor_scalar(prob[:, i % PR, 0:P * (i + 1)], prob[:, i % PR, 0:P * (i + 1)],
                                              rinv[:, i % 4:i % 4 + 1], None, ALU.mult).then_inc(pn_done, 1)
                    pipelined(dve, QB, HA, 1, slot)
                    for a in range(2):
                        dve.wait_ge(wo_mm, 2 * b + a + 1)
                        xs = xT[:, b * T + a * CH:b * T + (a + 1) * CH]
                        dve.scalar_tensor_tensor(out=xs, in0=scores[0][:, a * CH:(a + 1) * CH], scalar=bias[:, 3:4], in1=xs,
                                                 op0=ALU.add, op1=ALU.add).then_inc(res_done, 1)


def stack_semaphores(sem):
    names = """ld const_ld zeroed wqkv_ld wo_ld ffw_ld q_mm k_mm ssq_mm ssk_mm va_mm vs_ld
            s_mm t_mm pv_mm wo_mm sqq_done sqk_done rlq_done rlk_done rq_done rk_done va_cp exp_done
            pt_cp o_cp pq_done pk_done swap_ld addq_done addk_done qn_done kn_done smax_done ssub_done
            ssum_done rinv_done pn_done y_add y_start shift_done a_mm g_mm gelu_done h_done out_mm y_done
            bias_done x_done"""
    return {n: sem("b_" + n) for n in names.split()}


def stack(rep, ln_call, S, nc, w, c, bank, wide, xT, y, ident, identb, ln_eps, ss_eps, ss_back,
          ln_pe, ln_act, ln_dve, norm_done, cs, cen):
    with ExitStack() as st:
        def sb(name, shape, dt=F32):
            return st.enter_context(nc.sbuf_tensor(f"b{rep}_{name}", shape, dt))

        PAD = BLK
        xs = sb("xs", [P, N])
        rot = sb("rot", [P, 4, T])
        band = sb("band", [P, 2, 4 * KEYS], BF16)
        same = sb("same", [P, P])
        wqkv = sb("wqkv", [P, 2, 3, P])
        wo = sb("wo", [P, 2, P])
        qks = sb("qks", [P, 2])
        lng = sb("lng", [P, 2])
        w1 = sb("w1", [P, 2, FT * P])
        w2 = sb("w2", [P, FT, P])
        b1 = sb("b1", [P, 2, FT])
        b2 = sb("b2", [P, 1])
        sq = sb("sq", [P, 2, CH])
        rr = sb("rr", [P, 2, 2, CH])
        prc = sb("prc", [P, 2, 2, CH])
        prs = sb("prs", [P, 2, 2, CH])
        sws = sb("sws", [P, 2, 2, CH])
        qd = sb("qd", [P, 2, NB, 2, BLK])
        kr = sb("kr", [P, PAD + T])
        va = sb("va", [P, 1 + N // P, P])
        vs = sb("vs", [P, N // P, P])
        prob = sb("prob", [P, 4, NB, P])
        smx = sb("smx", [P, 2, NB])
        ssm = sb("ssm", [P, 2, NB])
        rinv = sb("rinv", [P, 2, NB])
        pT = sb("pT", [P, 2, 4, P])
        oT = sb("oT", [P, 2, NB, BLK])
        gel = sb("gel", [P, FT, CH])
        hid = sb("hid", [P, 2, FT, CH])

        L0 = DEPTH * rep
        U0 = 32 * L0

        def um(u, l):
            return 32 * l + 8 * u[0] + u[1], u[1] % 4

        def pair(u):
            return 2 * u[0] + u[1] // 4

        def at_bank(i):
            return bank[i] if i >= 4 else bank[i][:, :]

        with nc.Block() as block:
            @block.sync
            def _(sp):
                for dst, src in ((rot[:, :, :], c["rot"]), (band[:, :, :], c["band"]), (same[:, :], c["same_head"])):
                    sp.dma_start(dst, src).then_inc(S["const_ld"], 16)
                with sp.Fori(L0, L0 + DEPTH) as l:
                    li = l - L0

                    def load_qkv(p, used, buf=0, sp=sp, l=l, li=li):
                        sp.wait_ge(S["va_mm"], ONE + 32 * l + 4 * used)
                        sp.wait_ge(S["zeroed"], ONE + 9 * (rep + 1))
                        wq = w["L0_ffn_Wqkv"][li, :, :].rearrange("d (i q f) -> d i q f", i=3, f=P)
                        sp.dma_start(wqkv[:, buf, :, :], wq[:, :, p, :]).then_inc(S["wqkv_ld"], 16)

                    def load_wo(u, sp=sp, l=l, li=li):
                        p = pair(u)
                        if not (isinstance(p, int) and p < 2):
                            sp.wait_ge(S["wo_mm"], ONE + 32 * l + 4 * (p - 1))
                        sp.wait_ge(S["zeroed"], ONE + 9 * (rep + 1))
                        sp.dma_start(wo[:, u[1] // 4, :], w["L0_ffn_Wo"][li, bass.ts(p, P), :]).then_inc(S["wo_ld"], 16)
                    load_qkv(0, 0)
                    for i, nm in enumerate(("L0_ffn_q_scale", "L0_ffn_k_scale")):
                        for h in range(2):
                            sp.dma_start(qks[h * DH:(h + 1) * DH, i:i + 1], w[nm][li, :].rearrange("(p a) -> p a", a=1))\
                                .then_inc(S["ld"], 16)
                    f = "L0_ffn_"
                    ffw = []
                    for a in range(2):
                        ffw.append((w1[:, a, 0:FI], w[f + "W1"][li, :, a * FI:(a + 1) * FI]))
                        for i in range(FT):
                            r = P if i < FT - 1 else FR
                            ffw.append((b1[0:r, a, i:i + 1], w[f + "b1"][li, a * FI + i * P:a * FI + i * P + r]
                                        .rearrange("(p a) -> p a", a=1)))
                    ffw.append((w2[:, 0:FT - 1, :], w[f + "W2"][li, 0:(FT - 1) * P, :].rearrange("(i p) d -> p i d", p=P)))
                    ffw.append((w2[0:FR, FT - 1, :], w[f + "W2"][li, (FT - 1) * P:FI, :]))
                    for dst, nm in ((lng[:, 0:1], "ln_g"), (lng[:, 1:2], "ln_b"), (b2[:, 0:1], "b2")):
                        ffw.append((dst, w[f + nm][li, :].rearrange("(p a) -> p a", a=1)))

                    def slot(j, unit, sp=sp, l=l):
                        u = unit(0)
                        if u:
                            U, k = um(u, l)
                            sp.wait_ge(S["pk_done"], ONE + U + 1)
                            for h in range(4):
                                o = h ^ 1
                                sp.dma_start(sws[32 * o:32 * o + 32, k % 2, :, :], prs[32 * h:32 * h + 32, k % 2, :, :])\
                                    .then_inc(S["swap_ld"], 16)
                            if j % 4 == 0:
                                load_wo(u)
                            if j % 4 == 1 and not (isinstance(u[0], int) and pair(u) == PAIRS - 1):
                                load_qkv(pair(u) + 1, pair(u), buf=1 - j // 4)
                        u = unit(1)
                        if u:
                            U, k = um(u, l)
                            sp.wait_ge(S["va_cp"], ONE + U + 1)
                            sp.wait_ge(S["vs_ld"], ONE + 32 * U)
                            sp.dma_start(vs[0:BLK, 4 * k:4 * k + 4, :], va[BLK:P, 4 * k:4 * k + 4, :]).then_inc(S["vs_ld"], 16)
                            sp.dma_start(vs[BLK:P, 4 * k:4 * k + 4, :], va[0:BLK, 4 * k + 1:4 * k + 5, :]).then_inc(S["vs_ld"], 16)
                        if u and isinstance(u[0], int) and u[0] == 0:
                            sp.wait_ge(S["y_done"], ONE + NC * l)
                            sp.wait_ge(S["zeroed"], ONE + 9 * (rep + 1))
                            for dst, src in ffw[2 * (j - 1):2 * j]:
                                sp.dma_start(dst, src).then_inc(S["ffw_ld"], 16)
                    pipelined(sp, 8, PAIRS // 2, 1, slot, peel_last=True)

            @block.gpsimd
            def _(pool):
                if rep == 0:
                    for s in S.values():
                        pool.sem_inc(s, ONE)
                for t in (w1[:, :, :], w2[:, :, :], b1[:, :, :], qd[:, :, :, :, :], kr[:, 0:PAD], va[:, 0, :],
                          prob[:, :, :, 0:P - KEYS]):
                    pool.memset(t, 0.0).then_inc(S["zeroed"], 1)
                pool.wait_ge(S["zeroed"], ONE + 9 * rep + 7)
                for b in range(B):
                    pool.memset(xs[BLK:P, b * T:b * T + 1], 0.0).then_inc(S["zeroed"], 1)
                with pool.Fori(L0, L0 + DEPTH) as l:
                    def slot(j, unit, pool=pool, l=l):
                        u = unit(2)
                        if u:
                            U, k = um(u, l)
                            pool.wait_ge(S["rinv_done"], ONE + U + 1)
                            pool.tensor_tensor(prob[:, k, :, P - KEYS:P], prob[:, k, :, P - KEYS:P],
                                               rinv[:, k % 2, :].rearrange("p (b a) -> p b a", a=1).broadcast_to([P, NB, KEYS]),
                                               ALU.mult).then_inc(S["pn_done"], 1)
                        u = unit(0)
                        if u:
                            U, k = um(u, l)
                            pool.wait_ge(S["swap_ld"], ONE + 64 * (U + 1))
                            for i, nm in enumerate(("addq_done", "addk_done")):
                                pool.tensor_tensor(prc[:, k % 2, i, :], prc[:, k % 2, i, :], sws[:, k % 2, i, :], ALU.add)\
                                    .then_inc(S[nm], 1)
                    pipelined(pool, 8, PAIRS // 2, 3, slot)

            @block.tensor
            def _(pe):
                pe.wait_ge(S["const_ld"], ONE + 48 * (rep + 1))
                ln_pe(pe, ln_call, lambda k: xT[:, cs(k)])
                with pe.Fori(L0, L0 + DEPTH) as l:
                    def slot(j, unit, pe=pe, l=l):
                        a, b, d = unit(0), unit(1), unit(3)
                        if a:
                            U, k = um(a, l)
                            X = xs[:, cs(k)]
                            if k == 0:
                                pe.wait_ge(S["wqkv_ld"], ONE + 16 * (PAIRS * l + pair(a) + 1))
                            if isinstance(a[0], int) and a[0] == 0 and j < 4:
                                pe.wait_ge(S["shift_done"], ONE + 16 * l + 8 * rep + 2 * (k + 1))
                            W = wqkv[:, j // 4, :, :]
                            pe.wait_ge(S["pq_done"], ONE + U)
                            pe.matmul(bank[0][:, :], W[:, 0, :], X, start=True, stop=True).then_inc(S["q_mm"], 1)
                        if d:
                            UD, kd = um(d, l)
                            turn(pe, UD, kd, 0)
                        if a:
                            pe.wait_ge(S["va_cp"], ONE + U)
                            pe.matmul(bank[1][:, :], W[:, 1, :], X, start=True, stop=True).then_inc(S["k_mm"], 1)
                        if d:
                            values(pe, UD, kd, 0)
                        if a:
                            pe.wait_ge(S["sqq_done"], ONE + U + 1)
                            pe.wait_ge(S["y_add"], ONE + UD if d else 32 * l)
                            pe.matmul(bank[2][:, :], same[:, :], sq[:, 0, :], start=True, stop=True).then_inc(S["ssq_mm"], 1)
                        if d:
                            turn(pe, UD, kd, 1)
                        if b:
                            UB, kb = um(b, l)
                            first = kb % 2 == 0
                            pe.wait_ge(S["kn_done"], ONE + UB + 1)
                            pe.wait_ge(S["ssub_done"], ONE + UB)
                            for h in range(2):
                                s = wide[0][:, h * CH:h * CH + 4 * KEYS]
                                pe.matmul(s, identb[:, :], band[:, 0 if first and h == 0 else 1, :],
                                          start=True, stop=False, skip_group_check=True)
                                for i in range(4):
                                    n = 4 * h + i
                                    at = PAD + (kb % 2) * CH + n * BLK - WIN
                                    m = pe.matmul(s[:, i * KEYS:(i + 1) * KEYS], qd[:, kb % 2, n, :, :]
                                                  .rearrange("p h q -> p (h q)"), kr[:, at:at + KEYS],
                                                  start=False, stop=(i == 3), skip_group_check=True)
                            m.then_inc(S["s_mm"], 1)
                        if d:
                            values(pe, UD, kd, 1)
                        if a:
                            pe.wait_ge(S["sqk_done"], ONE + U + 1)
                            pe.wait_ge(S["rlk_done"], ONE + U)
                            pe.matmul(bank[3][:, :], same[:, :], sq[:, 1, :], start=True, stop=True).then_inc(S["ssk_mm"], 1)
                            pe.wait_ge(S["pk_done"], ONE + U + 1)
                            for t in range(4):
                                at = k * CH + t * P
                                m = pe.matmul(bank[1][:, t * P:(t + 1) * P], xs[:, at:at + P], W[:, 2, :],
                                              start=(t == 0), stop=(t == 3), skip_group_check=True)
                            m.then_inc(S["va_mm"], 1)
                        if d:
                            if kd == 0:
                                pe.wait_ge(S["wo_ld"], ONE + 16 * (PAIRS * l + pair(d) + 1))
                            pe.wait_ge(S["o_cp"], ONE + 4 * UD + 4)
                            if a:
                                pe.wait_ge(S["rlq_done"], ONE + U + 1)
                            else:
                                pe.wait_ge(S["rlq_done"], ONE + 32 * l + 32)
                                pe.wait_ge(S["y_add"], ONE + UD)
                            pe.matmul(bank[2][:, :], wo[:, d[1] // 4, :], oT[:, kd % 2, :, :].rearrange("p b q -> p (b q)"),
                                      start=True, stop=True).then_inc(S["wo_mm"], 1)

                    def turn(pe, UD, kd, h):
                        if h == 0:
                            pe.wait_ge(S["pn_done"], ONE + UD + 1)
                        pe.wait_ge(S["pt_cp"], ONE + 2 * UD + h)
                        for i in range(4):
                            m = pe.transpose(bank[6][:, i * P:(i + 1) * P], prob[:, kd, 4 * h + i, :], ident[:, :])
                        m.then_inc(S["t_mm"], 1)

                    def values(pe, UD, kd, h):
                        pe.wait_ge(S["pt_cp"], ONE + 2 * UD + h + 1)
                        pe.wait_ge(S["o_cp"], ONE + 4 * UD + 2 * h)
                        if h == 0:
                            pe.wait_ge(S["vs_ld"], ONE + 32 * (UD + 1))
                        for i in range(4):
                            n = 4 * h + i
                            v = va[:, 1 + 4 * kd + n // 2, :] if n % 2 else vs[:, 4 * kd + n // 2, :]
                            m = pe.matmul(bank[7][:, i * P:(i + 1) * P], v, pT[:, h, i, :],
                                          start=(i == 0), stop=(i == 3), skip_group_check=True)
                        m.then_inc(S["pv_mm"], 1)

                    pipelined(pe, 8, PAIRS // 2, 3, slot)


                    for name, count in (("va_cp", 32), ("pk_done", 32), ("rlk_done", 32),
                                        ("ssub_done", 32), ("pt_cp", 64), ("o_cp", 128)):
                        pe.wait_ge(S[name], ONE + count * (l + 1))

                    def ready(pe, k, l=l):
                        pe.wait_ge(S["shift_done"], ONE + 16 * l + 8 * rep + 8 + 2 * (k + 1))
                        if k == 2:
                            pe.wait_ge(S["y_add"], ONE + 32 * (l + 1))
                    ln_pe(pe, ln_call + 1 + (l - L0), lambda k: xs[:, cs(k)], ready)
                    pe.wait_ge(S["ffw_ld"], ONE + 208 * (l + 1))

                    def up(k, pe=pe, l=l):
                        pe.wait_ge(S["bias_done"], ONE + NC * l + k + 1)
                        for i in range(FT):
                            if k:
                                pe.wait_ge(S["h_done"], ONE + FT * (NC * l + k - 1) + i + 1)
                            for a, nm in enumerate(("a_mm", "g_mm")):
                                pe.matmul(at_bank(2 * i + a), w1[:, a, i * P:(i + 1) * P], cen[:, k, :],
                                          start=True, stop=True).then_inc(S[nm], 1)
                    up(0)
                    for k in range(NC):
                        if k + 1 < NC:
                            up(k + 1)
                        pe.wait_ge(S["h_done"], ONE + FT * (NC * l + k + 1))
                        if k >= 2:
                            pe.wait_ge(S["y_done"], ONE + NC * l + k - 1)
                        for i in range(FT):
                            m = pe.matmul(bank[6 + k % 2], w2[:, i, :], hid[:, k % 2, i, :], start=(i == 0), stop=(i == FT - 1))
                        m.then_inc(S["out_mm"], 1)

            @block.scalar
            def _(act):
                ln_act(act, ln_call)
                with act.Fori(L0, L0 + DEPTH) as l:
                    act.preload_act_table_set("natural_log_exp_and_others")
                    def slot(j, unit, act=act, l=l):
                        a, b, d = unit(0), unit(1), unit(3)

                        def turned(h):
                            act.wait_ge(S["t_mm"], ONE + 2 * UD + h + 1)
                            act.activation(pT[:, h, :, :], bank[6].rearrange("p (i q) -> p i q", i=4), ACT.Copy)\
                                .then_inc(S["pt_cp"], 1)

                        def outputs(h):
                            act.wait_ge(S["pv_mm"], ONE + 2 * UD + h + 1)
                            o = bank[7].rearrange("p (i h q) -> p i h q", i=4, h=2)
                            for e in range(2):
                                act.activation(oT[e * DH:(e + 1) * DH, kd % 2, 4 * h:4 * h + 4, :],
                                               o[e * DH:(e + 1) * DH, :, e, :], ACT.Copy).then_inc(S["o_cp"], 1)

                        def inverse_norm(i, mm, ln, done):
                            act.wait_ge(S[mm], ONE + U + 1)
                            act.activation(rr[:, k % 2, i, :], bank[2 + i][:, :], ACT.Ln, bias=ss_eps[:, 0:1], scale=SS_SCALE)\
                                .then_inc(S[ln], 1)
                            act.wait_ge(S[ln], ONE + U + 1)
                            act.activation(rr[:, k % 2, i, :], rr[:, k % 2, i, :], ACT.Exp, bias=ss_back[:, 0:1], scale=-0.5)\
                                .then_inc(S[done], 1)
                        if a:
                            U, k = um(a, l)
                            act.wait_ge(S["q_mm"], ONE + U + 1)
                            act.activation(sq[:, 0, :], bank[0][:, :], ACT.Square).then_inc(S["sqq_done"], 1)
                        if d:
                            UD, kd = um(d, l)
                            turned(0)
                        if a:
                            act.wait_ge(S["k_mm"], ONE + U + 1)
                            act.activation(sq[:, 1, :], bank[1][:, :], ACT.Square).then_inc(S["sqk_done"], 1)
                        if d:
                            outputs(0)
                        if a:
                            inverse_norm(0, "ssq_mm", "rlq_done", "rq_done")
                        if d:
                            turned(1)
                            outputs(1)
                        if b:
                            UB, kb = um(b, l)
                            act.wait_ge(S["ssub_done"], ONE + UB + 1)
                            act.activation(prob[:, kb, :, P - KEYS:P], prob[:, kb, :, P - KEYS:P], ACT.Exp, scale=QK_SCALE)\
                                .then_inc(S["exp_done"], 1)
                        if a:
                            inverse_norm(1, "ssk_mm", "rlk_done", "rk_done")
                            act.wait_ge(S["va_mm"], ONE + U + 1)
                            act.activation(va[:, 4 * k + 1:4 * k + 5, :], bank[1][:, :].rearrange("p (t d) -> p t d", t=4), ACT.Copy)\
                                .then_inc(S["va_cp"], 1)
                    pipelined(act, 8, PAIRS // 2, 3, slot)

                    def shift_by_b(act, k, l=l):
                        act.wait_ge(norm_done, NC * (ln_call + 1 + (l - L0)) + k + 1)
                        act.activation(cen[:, k, :], cen[:, k, :], ACT.Identity, bias=lng[:, 1:2])\
                            .then_inc(S["bias_done"], 1)
                    ln_act(act, ln_call + 1 + (l - L0), shift_by_b)
                    for k in range(NC):
                        for i in range(FT):
                            n = FT * (NC * l + k) + i
                            act.wait_ge(S["g_mm"], ONE + n + 1)
                            if k:
                                act.wait_ge(S["h_done"], ONE + n - FT + 1)
                            act.activation(gel[:, i, :], at_bank(2 * i + 1), ACT.Gelu, bias=b1[:, 1, i:i + 1])\
                                .then_inc(S["gelu_done"], 1)

            @block.vector
            def _(dve):
                dve.wait_ge(S["zeroed"], ONE + 9 * (rep + 1))
                dve.wait_ge(S["const_ld"], ONE + 48 * (rep + 1))
                ln_dve(dve, ln_call, lambda k: xT[:, cs(k)], lambda k: y[:, cs(k)])
                dve.wait_ge(norm_done, NC * (ln_call + 1))

                def shift(k):
                    dve.tensor_copy(xs[0:BLK, cs(k)], y[0:BLK, cs(k)]).then_inc(S["shift_done"], 1)
                    lo = k * CH + (k * CH % T == 0)
                    dve.tensor_copy(xs[BLK:P, lo:(k + 1) * CH], y[BLK:P, lo - 1:(k + 1) * CH - 1]).then_inc(S["shift_done"], 1)

                for k in range(NC):
                    shift(k)
                with dve.Fori(L0, L0 + DEPTH) as l:
                    dve.wait_ge(S["ld"], ONE + 64 * (l + 1))

                    def slot(j, unit, dve=dve, l=l):
                        a, b, c_, d = unit(0), unit(1), unit(2), unit(3)
                        if c_:
                            UC, kc = um(c_, l)
                            dve.wait_ge(S["exp_done"], ONE + UC + 1)
                            dve.tensor_reduce(ssm[:, kc % 2, :], prob[:, kc, :, P - KEYS:P], AX.X, ALU.add)\
                                .then_inc(S["ssum_done"], 1)
                            dve.wait_ge(S["ssum_done"], ONE + UC + 1)
                            dve.reciprocal(rinv[:, kc % 2, :], ssm[:, kc % 2, :]).then_inc(S["rinv_done"], 1)
                        if b:
                            UB, kb = um(b, l)
                            dve.wait_ge(S["addq_done"], ONE + UB + 1)
                            dve.wait_ge(S["rq_done"], ONE + UB + 1)
                            for h in range(2):
                                hs = slice(h * DH, (h + 1) * DH)
                                dve.tensor_tensor(qd[hs, kb % 2, :, h, :],
                                                  prc[hs, kb % 2, 0, :].rearrange("p (n q) -> p n q", n=NB),
                                                  rr[hs, kb % 2, 0, :].rearrange("p (n q) -> p n q", n=NB), ALU.mult)\
                                    .then_inc(S["qn_done"], 1)
                            dve.wait_ge(S["addk_done"], ONE + UB + 1)
                            dve.wait_ge(S["rk_done"], ONE + UB + 1)
                            at = PAD + (kb % 2) * CH
                            dve.tensor_tensor(kr[:, at:at + CH], prc[:, kb % 2, 1, :], rr[:, kb % 2, 1, :], ALU.mult)\
                                .then_inc(S["kn_done"], 1)
                        if a:
                            U, k = um(a, l)
                            t = slice((k % 2) * CH, (k % 2 + 1) * CH)
                            for i, sqd, done in ((0, "sqq_done", "pq_done"), (1, "sqk_done", "pk_done")):
                                dve.wait_ge(S[sqd], ONE + U + 1)
                                for o, r in ((prc, 0), (prs, 1)):
                                    m = dve.scalar_tensor_tensor(out=o[:, k % 2, i, :], in0=bank[i][:, :], scalar=qks[:, i:i + 1],
                                                                 in1=rot[:, 2 * i + r, t], op0=ALU.mult, op1=ALU.mult)
                                m.then_inc(S[done], 1)
                        if b:
                            sc = wide[0][:, :].rearrange("p (h c) -> p h c", h=2)[:, :, 0:4 * KEYS]\
                                .rearrange("p h (i k) -> p h i k", k=KEYS)
                            dve.wait_ge(S["s_mm"], ONE + UB + 1)
                            dve.tensor_reduce(smx[:, kb % 2, :], sc, AX.X, ALU.max).then_inc(S["smax_done"], 1)
                            dve.wait_ge(S["smax_done"], ONE + UB + 1)
                            dve.tensor_tensor(prob[:, kb, :, P - KEYS:P].rearrange("p (h i) k -> p h i k", h=2), sc,
                                              smx[:, kb % 2, :].rearrange("p (h i a) -> p h i a", h=2, a=1)
                                              .broadcast_to([P, 2, 4, KEYS]), ALU.subtract).then_inc(S["ssub_done"], 1)
                        if d:
                            UD, kd = um(d, l)
                            dve.wait_ge(S["wo_mm"], ONE + UD + 1)
                            dve.tensor_tensor(y[:, cs(kd)], bank[2][:, :], y[:, cs(kd)], ALU.add).then_inc(S["y_add"], 1)
                            if isinstance(d[0], int) and j < 3:
                                dve.wait_ge(S["y_add"], ONE + UD + 1)
                                for i in ((0, 1) if kd == 1 else (kd,)):
                                    shift(i)
                    pipelined(dve, 8, PAIRS // 2, 3, slot)
                    dve.wait_ge(S["shift_done"], ONE + 16 * l + 8 * rep + 16)
                    dve.wait_ge(S["ffw_ld"], ONE + 208 * (l + 1))
                    ln_dve(dve, ln_call + 1 + (l - L0), lambda k: xs[:, cs(k)],
                           lambda k: cen[:, k, :], gain=lng[:, 0:1])

                    def hidden(k, dve=dve, l=l):
                        for i in range(FT):
                            n = FT * (NC * l + k) + i
                            dve.wait_ge(S["a_mm"], ONE + n + 1)
                            dve.wait_ge(S["gelu_done"], ONE + n + 1)
                            if k >= 2:
                                dve.wait_ge(S["out_mm"], ONE + NC * l + k - 1)
                            dve.scalar_tensor_tensor(out=hid[:, k % 2, i, :], in0=at_bank(2 * i), scalar=b1[:, 0, i:i + 1],
                                                     in1=gel[:, i, :], op0=ALU.add, op1=ALU.mult).then_inc(S["h_done"], 1)
                    hidden(0)
                    for k in range(NC):
                        if k + 1 < NC:
                            hidden(k + 1)
                        dve.wait_ge(S["out_mm"], ONE + NC * l + k + 1)
                        dve.scalar_tensor_tensor(out=y[:, cs(k)], in0=bank[6 + k % 2], scalar=b2[:, 0:1], in1=y[:, cs(k)],
                                                 op0=ALU.add, op1=ALU.add).then_inc(S["y_done"], 1)
                        dve.wait_ge(S["y_done"], ONE + NC * l + k + 1)
                        shift(k)
                dve.wait_ge(S["y_done"], ONE + NC * (L0 + DEPTH))
                for k in range(NC):
                    dve.tensor_tensor(xT[:, cs(k)], xT[:, cs(k)], y[:, cs(k)], ALU.add).then_inc(S["x_done"], 1)


def stage_c(nc, w, c, sem, bank, wide, xT, y, ident, jmean, ln_eps, sqr, rstd, ln_pe, ln_act, ln_dve, norm_done, cs, ln_call):
    with ExitStack() as st:
        def sb(name, shape, dt=F32):
            return st.enter_context(nc.sbuf_tensor("c_" + name, shape, dt))

        names = ["w_q", "w_k", "w_v", "w_f", "w_o"]
        wtok = sb("wtok", [P, 5, D])
        wT = sb("wT", [P, 5, D])
        gains = sb("gains", [P, 2])
        hmask = sb("hmask", [P, HG])
        pick = sb("pick", [P, KG, P])
        put = sb("put", [P, KG, P])
        spread = sb("spread", [P, P])
        qkv = sb("qkv", [P, 3, N])
        f = sb("f", [P, N])
        e = sb("e", [P, N])
        s = sb("s", [P, N])
        oT = sb("oT", [P, N])
        own = sb("own", [P, 4, T])
        hi = sb("hi", [P, 3, T], F32R)
        lo = sb("lo", [P, 3, T], F32R)
        pickr = sb("pickr", [P, KG, P], F32R)
        srep = sb("srep", [P, T])
        lrep = sb("lrep", [P, T])
        inp = sb("inp", [P, 2, T])
        stt = sb("stt", [P, 2, T])
        prod = sb("prod", [P, 2, T])
        zs = sb("zs", [P, T])
        pm = sb("pm", [P, QB, DG])
        mx = sb("mx", [P, QB])
        sm = sb("sm", [P, QB])
        ri = sb("ri", [P, QB])
        prr = sb("prr", [P, QB, KK, DG])
        prep = sb("prep", [P, T])

        ld, wt_mm, wt_cp = sem("c_ld"), sem("c_wt_mm"), sem("c_wt_cp")
        rsq_done, rms_mm, rln_done, rrs_done, rms_done = (sem("c_rsq_done"), sem("c_rms_mm"), sem("c_rln_done"),
                                                          sem("c_rrs_done"), sem("c_rms_done"))
        pr_mm, pr_cp, f_step = sem("c_pr_mm"), sem("c_pr_cp"), sem("c_f_step")

        def rms_act(act, n, src):
            act.preload_act_table_set("natural_log_exp_and_others")
            for k in range(NC):
                act.activation(sqr[:, k, :], src(k), ACT.Square).then_inc(rsq_done, 1)
            for k in range(NC):
                act.wait_ge(rms_mm, NC * n + k + 1)
                act.activation(rstd[:, k, :], bank[4 + k], ACT.Ln, bias=ln_eps[:, 0:1]).then_inc(rln_done, 1)
            for k in range(NC):
                act.wait_ge(rln_done, NC * n + k + 1)
                act.activation(rstd[:, k, :], rstd[:, k, :], ACT.Exp, scale=-0.5).then_inc(rrs_done, 1)

        def rms_pe(pe, n):
            for k in range(NC):
                pe.wait_ge(rsq_done, NC * n + k + 1)
                pe.matmul(bank[4 + k], jmean[:, :], sqr[:, k, :], start=True, stop=True).then_inc(rms_mm, 1)

        def rms_dve(dve, n, t):
            for k in range(NC):
                dve.wait_ge(rrs_done, NC * n + k + 1)
                dve.scalar_tensor_tensor(out=t(k), in0=t(k), scalar=gains[:, n:n + 1], in1=rstd[:, k, :],
                                         op0=ALU.mult, op1=ALU.mult).then_inc(rms_done, 1)

        with nc.Block() as block:
            @block.sync
            def _(sp):
                for i, nm in enumerate(names):
                    sp.dma_start(wtok[:, i, :], w["L0_attn_b_" + nm]).then_inc(ld, 16)
                for i, nm in enumerate(("norm_weight", "gnorm_weight")):
                    sp.dma_start(gains[:, i:i + 1], w["L0_attn_b_" + nm].rearrange("(p a) -> p a", a=1)).then_inc(ld, 16)
                for dst, nm in ((hmask[:, :], "c_hmask"), (pick[:, :, :], "c_pick"), (put[:, :, :], "c_put"),
                                (spread[:, :], "c_spread")):
                    sp.dma_start(dst, c[nm]).then_inc(ld, 16)

            @block.tensor
            def _(pe):
                ln_pe(pe, ln_call, lambda k: xT[:, cs(k)])
                rms_pe(pe, 0)
                pe.wait_ge(ld, 16 * 11)
                for i in range(5):
                    o = bank[i // 4]
                    m = pe.transpose(o[:, (i % 4) * P:(i % 4 + 1) * P], wtok[:, i, :], ident[:, :])
                m.then_inc(wt_mm, 1)
                pe.wait_ge(wt_cp, 2)
                pe.wait_ge(rms_done, NC)
                for k in range(NC):
                    for i in range(4):
                        if k:
                            pe.wait_ge(pr_cp, 4 * (k - 1) + i + 1)
                        pe.matmul(bank[i][:, :], wT[:, i, :], y[:, cs(k)], start=True, stop=True).then_inc(pr_mm, 1)

            @block.scalar
            def _(act):
                ln_act(act, ln_call)
                act.wait_ge(norm_done, NC * (ln_call + 1))
                rms_act(act, 0, lambda k: y[:, cs(k)])
                act.wait_ge(wt_mm, 1)
                act.activation(wT[:, 0:4, :], bank[0][:, :].rearrange("p (i d) -> p i d", i=4), ACT.Copy).then_inc(wt_cp, 1)
                act.activation(wT[:, 4, :], bank[1][:, 0:P], ACT.Copy).then_inc(wt_cp, 1)
                for k in range(NC):
                    for i in range(4):
                        act.wait_ge(pr_mm, 4 * k + i + 1)
                        if i < 3:
                            act.activation(qkv[:, i, cs(k)], bank[i][:, :], ACT.Silu).then_inc(pr_cp, 1)
                        else:
                            act.activation(f[:, cs(k)], bank[i][:, :], ACT.Copy).then_inc(pr_cp, 1)
                act.wait_ge(pr_cp, 4 * NC)
                act.activation(e[:, :], f[:, :], ACT.Abs).then_inc(f_step, 1)
                act.wait_ge(f_step, 1)
                act.activation(e[:, :], e[:, :], ACT.Exp, scale=-1.0).then_inc(f_step, 1)
                act.wait_ge(f_step, 2)
                act.activation(e[:, :], e[:, :], ACT.Ln, bias=1.0).then_inc(f_step, 1)
                act.wait_ge(f_step, 4)
                act.activation(e[:, :], f[:, :], ACT.Tanh, scale=-1.0 / 32).then_inc(f_step, 1)

            @block.vector
            def _(dve):
                ln_dve(dve, ln_call, lambda k: xT[:, cs(k)], lambda k: y[:, cs(k)])
                dve.wait_ge(norm_done, NC * (ln_call + 1))
                dve.wait_ge(ld, 16 * 11)
                rms_dve(dve, 0, lambda k: y[:, cs(k)])
                dve.memset(oT[:, :], 0.0)
                dve.tensor_copy(pickr[:, :, :], pick[:, :, :])
                dve.wait_ge(f_step, 3)
                dve.scalar_tensor_tensor(out=f[:, :], in0=f[:, :], scalar=0.0, in1=e[:, :], op0=ALU.min,
                                         op1=ALU.subtract).then_inc(f_step, 1)
                dve.wait_ge(f_step, 5)
                dve.tensor_scalar(f[:, :], e[:, :], 1.0, None, ALU.add).then_inc(f_step, 1)
                dve.wait_ge(f_step, 6)
                dve.reciprocal(f[:, :], f[:, :]).then_inc(f_step, 1)
                dve.wait_ge(f_step, 7)
                dve.scalar_tensor_tensor(out=s[:, :], in0=e[:, :], scalar=2.0, in1=f[:, :], op0=ALU.mult,
                                         op1=ALU.mult).then_inc(f_step, 1)

        hi_done, lo_done = sem("c_hi_done"), sem("c_lo_done")
        own_done, rep_mm, rep_cp = sem("c_own_done"), sem("c_rep_mm"), sem("c_rep_cp")
        in_mm, in_done, scan_done, qb_mm, prod_done, red_mm = (sem("c_in_mm"), sem("c_in_done"), sem("c_scan_done"),
                                                               sem("c_qb_mm"), sem("c_prod_done"), sem("c_red_mm"))
        z_cp, zt_mm, p_step, pt_mm, prep_done, acc_done = (sem("c_z_cp"), sem("c_zt_mm"), sem("c_p_step"), sem("c_pt_mm"),
                                                           sem("c_prep_done"), sem("c_acc_done"))
        R = 2 * KG
        with nc.Block() as block:
            @block.gpsimd
            def _(pool):
                for t in (in_done, prod_done, acc_done, in_mm, scan_done):
                    pool.sem_inc(t, ONE)
                with pool.Fori(0, B) as b:
                    with pool.Fori(0, HG) as h:
                        g = b * HG + h
                        for i in range(3):
                            pool.wait_ge(hi_done, 3 * g + i + 1)
                            pool.tensor_tensor(lo[:, i, :], own[:, i, :], hi[:, i, :], ALU.subtract).then_inc(lo_done, 1)

            @block.tensor
            def _(pe):
                with pe.Fori(0, B) as b:
                    with pe.Fori(0, HG) as h:
                        g = b * HG + h
                        pe.wait_ge(own_done, 4 * g + 4)
                        pe.wait_ge(hi_done, 3 * g + 3)
                        pe.wait_ge(lo_done, 3 * g + 3)
                        pe.wait_ge(acc_done, ONE + 2 * g)
                        for a in range(2):
                            pe.matmul(bank[2 + a][:, :], spread[:, :], own[:, 3, cs(a)], start=True, stop=True).then_inc(rep_mm, 1)

                        def enter(r, pe=pe, g=g):
                            pe.wait_ge(in_done, ONE + R * g + r)
                            for a in range(2):
                                for part in (hi, lo):
                                    m = pe.matmul(bank[4 + a], pickr[:, r % KG, :], part[:, 1 if r < KG else 2, cs(a)],
                                                  start=(part is hi), stop=(part is lo))
                            m.then_inc(in_mm, 1)

                        def query(r, pe=pe, g=g):
                            pe.wait_ge(prod_done, ONE + R * g + r)
                            for a in range(2):
                                for part in (hi, lo):
                                    m = pe.matmul(bank[6 + a], pickr[:, r, :], part[:, 0, cs(a)],
                                                  start=(part is hi), stop=(part is lo))
                            m.then_inc(qb_mm, 1)

                        def gather(r, pe=pe, g=g):
                            pe.wait_ge(prod_done, ONE + R * g + r + 1)
                            for a in range(2):
                                m = pe.matmul(bank[a][:, :], spread[:, :] if r < KG else put[:, r % KG, :], prod[:, r % 2, cs(a)],
                                              start=(r % KG == 0), stop=(r % KG == KG - 1), skip_group_check=True)
                            m.then_inc(red_mm, 1)
                        enter(0)
                        query(0)
                        for r in range(KG):
                            enter(r + 1)
                            if r + 1 < KG:
                                query(r + 1)
                            gather(r)
                        pe.wait_ge(z_cp, 2 * g + 2)
                        pe.wait_ge(rep_cp, 4 * g + 4)
                        for i in range(QB):
                            m = pe.transpose(bank[2 + i // 4][:, (i % 4) * P:(i % 4 + 1) * P], zs[:, i * P:(i + 1) * P], ident[:, :])
                        m.then_inc(zt_mm, 1)
                        pe.wait_ge(p_step, 6 * g + 6)
                        for i in range(QB):
                            m = pe.transpose(bank[2 + i // 4][:, (i % 4) * P:(i % 4 + 1) * P],
                                             prr[:, i, :, :].rearrange("p k m -> p (k m)"), ident[:, :])
                        m.then_inc(pt_mm, 1)
                        for r in range(KG, R):
                            if r + 1 < R:
                                enter(r + 1)
                            gather(r)

            @block.scalar
            def _(act):
                act.sem_inc(red_mm, 2)
                with act.Fori(0, B) as b:
                    with act.Fori(0, HG) as h:
                        g = b * HG + h
                        act.wait_ge(in_mm, ONE + R * g)
                        for i in range(4):
                            src = qkv[:, i, bass.ds(b * T, T)] if i < 3 else s[:, bass.ds(b * T, T)]
                            act.activation(own[:, i, :], src, ACT.Copy, scale=hmask[:, bass.ds(h, 1)]).then_inc(own_done, 1)
                        for i in range(3):
                            act.wait_ge(own_done, 4 * g + i + 1)
                            act.activation(hi[:, i, :], own[:, i, :], ACT.Copy).then_inc(hi_done, 1)
                        act.wait_ge(scan_done, ONE + R * g)
                        for a in range(2):
                            act.wait_ge(rep_mm, 2 * g + a + 1)
                            act.activation(srep[:, cs(a)], bank[2 + a][:, :], ACT.Copy).then_inc(rep_cp, 1)
                            act.activation(lrep[:, cs(a)], bank[2 + a][:, :], ACT.Identity, bias=1.0, scale=-1.0).then_inc(rep_cp, 1)
                        act.wait_ge(red_mm, R * g + KG + 2)
                        for a in range(2):
                            act.activation(zs[:, cs(a)], bank[a][:, :], ACT.Copy).then_inc(z_cp, 1)
                        act.wait_ge(p_step, 6 * g + 2)
                        act.activation(pm[:, :, :], pm[:, :, :], ACT.Exp).then_inc(p_step, 1)
                        act.wait_ge(pt_mm, g + 1)
                        for a in range(2):
                            act.activation(prep[:, cs(a)], bank[2 + a][:, :], ACT.Copy).then_inc(prep_done, 1)

            @block.vector
            def _(dve):
                with dve.Fori(0, B) as b:
                    with dve.Fori(0, HG) as h:
                        g = b * HG + h
                        dve.wait_ge(rep_cp, 4 * g + 4)

                        def tile(r, dve=dve, g=g):
                            n = R * g + r
                            dve.wait_ge(in_mm, ONE + n + 1)
                            dve.tensor_tensor(inp[:, r % 2, :], wide[0][:, :], srep[:, :], ALU.mult).then_inc(in_done, 1)
                            dve.wait_ge(in_done, ONE + n + 1)
                            dve.tensor_tensor_scan(stt[:, r % 2, :], lrep[:, :], inp[:, r % 2, :], 0.0, ALU.mult, ALU.add)\
                                .then_inc(scan_done, 1)
                            if r < KG:
                                dve.wait_ge(qb_mm, KG * g + r + 1)
                            elif r == KG:
                                dve.wait_ge(prep_done, 2 * g + 2)
                            dve.wait_ge(red_mm, n + 1)
                            dve.wait_ge(scan_done, ONE + n + 1)
                            dve.tensor_tensor(prod[:, r % 2, :], wide[1][:, :] if r < KG else prep[:, :], stt[:, r % 2, :],
                                              ALU.mult).then_inc(prod_done, 1)
                        for r in range(KG):
                            tile(r)
                        dve.wait_ge(zt_mm, g + 1)
                        for a in range(2):
                            z = bank[2 + a][:, :].rearrange("p (i c) -> p i c", i=4)[:, :, 0:DG]
                            m = dve.tensor_reduce(mx[:, 4 * a:4 * a + 4], z, AX.X, ALU.max)
                        m.then_inc(p_step, 1)
                        dve.wait_ge(p_step, 6 * g + 1)
                        for a in range(2):
                            z = bank[2 + a][:, :].rearrange("p (i c) -> p i c", i=4)[:, :, 0:DG]
                            m = dve.tensor_tensor(pm[:, 4 * a:4 * a + 4, :], z, mx[:, 4 * a:4 * a + 4].rearrange("p (i a) -> p i a", a=1)
                                                  .broadcast_to([P, 4, DG]), ALU.subtract)
                        m.then_inc(p_step, 1)
                        dve.wait_ge(p_step, 6 * g + 3)
                        dve.tensor_reduce(sm[:, :], pm[:, :, :], AX.X, ALU.add).then_inc(p_step, 1)
                        dve.wait_ge(p_step, 6 * g + 4)
                        dve.reciprocal(ri[:, :], sm[:, :]).then_inc(p_step, 1)
                        dve.wait_ge(p_step, 6 * g + 5)
                        for k in range(KK):
                            m = dve.tensor_tensor(prr[:, :, k, :], pm[:, :, :], ri[:, :].rearrange("p (i a) -> p i a", a=1)
                                                  .broadcast_to([P, QB, DG]), ALU.mult)
                        m.then_inc(p_step, 1)
                        for r in range(KG, R):
                            tile(r)
                        dve.wait_ge(red_mm, R * g + R + 2)
                        for a in range(2):
                            o = oT[:, bass.ds(b * T + a * CH, CH)]
                            dve.scalar_tensor_tensor(out=o, in0=bank[a][:, :], scalar=hmask[:, bass.ds(h, 1)], in1=o,
                                                     op0=ALU.mult, op1=ALU.add).then_inc(acc_done, 1)

        sw_done, o_mm, o_add = sem("c_sw_done"), sem("c_o_mm"), sem("c_o_add")
        with nc.Block() as block:
            @block.scalar
            def _(act):
                for k in range(NC):
                    act.activation(oT[:, cs(k)], oT[:, cs(k)], ACT.Silu).then_inc(sw_done, 1)
                act.wait_ge(sw_done, NC)
                rms_act(act, 1, lambda k: oT[:, cs(k)])

            @block.tensor
            def _(pe):
                rms_pe(pe, 1)
                for k in range(NC):
                    pe.wait_ge(rms_done, NC + k + 1)
                    pe.matmul(bank[k][:, :], wT[:, 4, :], oT[:, cs(k)], start=True, stop=True).then_inc(o_mm, 1)

            @block.vector
            def _(dve):
                dve.wait_ge(sw_done, NC)
                rms_dve(dve, 1, lambda k: oT[:, cs(k)])
                for k in range(NC):
                    dve.wait_ge(o_mm, k + 1)
                    dve.tensor_tensor(xT[:, cs(k)], bank[k][:, :], xT[:, cs(k)], ALU.add).then_inc(o_add, 1)


def constants():
    import numpy as np
    bf = np.dtype("bfloat16")
    t = {"ident": np.eye(P, dtype=np.float32), "identb": np.eye(P).astype(bf),
         "jmean": np.full((P, P), 1 / D, np.float32)}
    head = np.arange(D) // (D // HA)
    own = (head[:, None] == np.arange(HA)[None, :])
    t["a_hmask"] = (own * D ** -0.5).astype(np.float32)
    t["a_cmask"] = np.broadcast_to(own.T[None], (P, HA, D)).astype(np.float32)
    i = np.arange(P)
    t["a_dmask"] = np.where(i[:, None] >= i[None, :], 0.0, NEG).astype(bf)
    half = np.arange(0, DH, 2, dtype=np.float32)
    inv = (1.0 / 10000.0 ** (half / DH)).astype(np.float32)
    pos = np.arange(T, dtype=np.float32)
    ang = (pos[:, None] * inv[None, :]).astype(np.float32)
    ang = np.concatenate([ang, ang], -1).astype(np.float64)
    base = ((half + 0.4 * DH) / (1.4 * DH)).astype(np.float32)
    power = (pos - T // 2) / (WIN // 2)
    scale = base[None, :].astype(np.float64) ** power[:, None]
    scale = np.concatenate([scale, scale], -1)
    sign = np.where(np.arange(DH) < DH // 2, 1.0, -1.0)
    tabs = [np.cos(ang) * scale, np.sin(ang) * scale * sign, np.cos(ang) / scale, np.sin(ang) / scale * sign]
    t["rot"] = np.stack([np.concatenate([x.T, x.T], 0) for x in tabs], 1).astype(np.float32).copy()
    blk = np.arange(P) // DH
    t["same_head"] = (blk[:, None] == blk[None, :]).astype(np.float32)
    q, k = np.arange(P)[:, None] % BLK, np.arange(KEYS)[None, :] - WIN
    seen = (q >= k) & (q - k <= WIN)
    m = np.where(seen, 0.0, NEG)
    m0 = np.where(seen & (k >= 0), 0.0, NEG)
    t["band"] = np.stack([np.concatenate([m0, m, m, m], 1), np.concatenate([m] * 4, 1)], 1).astype(bf).copy()
    f = np.arange(P)
    t["c_hmask"] = (f[:, None] // DG == np.arange(HG)[None, :]).astype(np.float32)
    t["c_pick"] = np.stack([(f[:, None] % DG == KK * g + f[None, :] // DG) for g in range(KG)], 1).astype(np.float32).copy()
    t["c_put"] = np.stack([(f[None, :] % DG == KK * g + f[:, None] // DG) for g in range(KG)], 1).astype(np.float32).copy()
    t["c_spread"] = (f[:, None] % DG == f[None, :] % DG).astype(np.float32)
    return t


def kernel(**inputs):
    import numpy as _np
    import concourse.bacc as _bacc
    from concourse import mybir as _mybir
    from concourse.bass_utils import run_bass_kernel_spmd as _run

    nc = _bacc.Bacc("TRN2", target_bir_lowering=False, num_devices=1)
    arrays, w, c = {}, {}, {}
    for group, named in ((w, inputs), (c, constants())):
        for name, a in named.items():
            a = _np.ascontiguousarray(a)
            arrays[f"in_{name}"] = a
            group[name] = nc.dram_tensor(f"in_{name}", a.shape, _mybir.dt.from_np(a.dtype), kind="ExternalInput").ap()
    out = nc.dram_tensor("out_0", (B, T, D), _mybir.dt.float32, kind="ExternalOutput").ap()
    hybrid_kernel(nc, w, c, out)
    r = _run(nc, [arrays], core_ids=[0])
    return r.results[0]["out_0"]
```
